# Optimizing a Trainium2 kernel written in Bass

```python
import numpy as np
import jax
import jax.numpy as jnp

def _softmax(x, axis=-1):
    return jax.nn.softmax(x, axis=axis)

def _gelu(x):
    return jax.nn.gelu(x, approximate=True)

def _silu(x):
    return jax.nn.silu(x)

def _sigmoid(x):
    return jax.nn.sigmoid(x)

def _layernorm(x, axis=-1, eps=1e-05):
    m = jnp.mean(x, axis=axis, keepdims=True)
    v = jnp.var(x, axis=axis, keepdims=True)
    return (x - m) / jnp.sqrt(v + eps)

def _scatter_add(tgt, idx, src, axis=0):
    return tgt.at[idx].add(src)

def _segment_sum(src, seg, n):
    return jax.ops.segment_sum(src, seg, n)
kernel_name = 'mk_gnn_preln_d2_gnn_r8_4fd009'

def setup_inputs(seed: int=0):
    np.random.seed(seed)
    _w = jnp.asarray

    def _rec_inputs():
        import jax
        import jax.numpy as jnp
        _gk = jax.random.key(seed)
        x = -0.0002117 + 1 * jax.random.normal(jax.random.fold_in(_gk, 1), (1250, 512), jnp.float32)
        _s = jax.random.randint(jax.random.fold_in(_gk, 2), (20000,), 0, 1250, jnp.int32)
        _d = jax.random.randint(jax.random.fold_in(_gk, 3), (20000,), 0, 1250, jnp.int32)
        _loop = jnp.arange(1250, dtype=jnp.int32)
        src = jnp.concatenate([_s, _d, _loop])
        dst = jnp.concatenate([_d, _s, _loop])
        _o = jnp.argsort(dst, stable=True)
        src = src[_o]
        dst = dst[_o]
        edge_attr_512 = -8.16379e-05 + 0.999858 * jax.random.normal(jax.random.fold_in(_gk, 12), (41250, 512), jnp.float32)
        return (x, src, dst, edge_attr_512)
    x, src, dst, edge_attr_512 = _rec_inputs()

    def _L0_gnn_setup():
        import jax, jax.numpy as jnp
        import numpy as np
        N_NODES = 6250
        N_EDGES = 50000
        IN_DIM = 512
        OUT_DIM = 512
        key = jax.random.key(seed)
        k1, k2, k3, k4 = jax.random.split(key, 4)
        x = jax.random.normal(k1, (N_NODES, IN_DIM), dtype=jnp.float32)
        edge_index = jax.random.randint(k2, (2, N_EDGES), 0, N_NODES, dtype=jnp.int64)
        W = jax.random.normal(k3, (OUT_DIM, IN_DIM), dtype=jnp.float32) / np.sqrt(IN_DIM)
        b = jax.random.normal(k4, (OUT_DIM,), dtype=jnp.float32) * 0.01
        return {'x': x, 'edge_index': edge_index, 'W': W, 'b': b}
    _L0_gnn_all = _L0_gnn_setup()
    _L0_gnn_in = {k: v for k, v in _L0_gnn_all.items() if k in ('W', 'b')}
    del _L0_gnn_all

    def _L1_gnn_setup():
        import jax, jax.numpy as jnp
        import numpy as np
        N_NODES = 2500
        N_EDGES = 25000
        N_SEG = 16
        EXTENT = 32
        N_PATHS = 64
        OP_SIZE = N_SEG * EXTENT
        key = jax.random.key(seed)
        k1, k2, k3, k4, k5, k6 = jax.random.split(key, 6)
        x_nodes = jax.random.normal(k1, (N_NODES, OP_SIZE), dtype=jnp.float32)
        x_edges = jax.random.normal(k2, (N_EDGES, OP_SIZE), dtype=jnp.float32)
        path_coeffs = jax.random.normal(k3, (N_PATHS,), dtype=jnp.float32)
        src = jax.random.randint(k4, (N_EDGES,), 0, N_NODES, dtype=jnp.int64)
        dst = jax.random.randint(k5, (N_EDGES,), 0, N_NODES, dtype=jnp.int64)
        path_indices = jax.random.randint(k6, (N_PATHS, 3), 0, N_SEG, dtype=jnp.int64)
        return {'x_nodes': x_nodes, 'x_edges': x_edges, 'path_coeffs': path_coeffs, 'src': src, 'dst': dst, 'path_indices': path_indices}
    _L1_gnn_all = _L1_gnn_setup()
    _L1_gnn_in = {k: v for k, v in _L1_gnn_all.items() if k in ('path_coeffs', 'path_indices')}
    del _L1_gnn_all
    return {'x': x, 'src': src, 'dst': dst, 'edge_attr_512': edge_attr_512, 'L0_gnn_W': _L0_gnn_in['W'], 'L0_gnn_b': _L0_gnn_in['b'], 'L1_gnn_path_coeffs': _L1_gnn_in['path_coeffs'], 'L1_gnn_path_indices': _L1_gnn_in['path_indices']}

def reference(x, src, dst, edge_attr_512, L0_gnn_W, L0_gnn_b, L1_gnn_path_coeffs, L1_gnn_path_indices):
    import jax
    import jax.numpy as jnp

    def _L0_gnn_ref(x, edge_index, W, b):
        import jax, jax.numpy as jnp
        import numpy as np
        N_NODES = 6250
        N_EDGES = 50000
        IN_DIM = 512
        OUT_DIM = 512
        n = x.shape[0]
        loops = jnp.arange(n, dtype=edge_index.dtype)
        row = jnp.concatenate([edge_index[0], loops])
        col = jnp.concatenate([edge_index[1], loops])
        deg = jax.ops.segment_sum(jnp.ones(row.shape[0], dtype=x.dtype), row, num_segments=n)
        dis = jax.lax.rsqrt(deg)
        norm = dis[row] * dis[col]
        h = x @ W.T + b
        out = jax.ops.segment_sum(norm[:, None] * h[row], col, num_segments=n)
        return jax.nn.relu(out)

    def _L1_gnn_ref(x_nodes, x_edges, path_coeffs, src, dst, path_indices):
        import jax, jax.numpy as jnp
        import numpy as np
        N_NODES = 2500
        N_EDGES = 25000
        N_SEG = 16
        EXTENT = 32
        N_PATHS = 64
        OP_SIZE = N_SEG * EXTENT
        n_nodes = x_nodes.shape[0]
        x1 = x_nodes[src].reshape(-1, N_SEG, EXTENT)
        x2 = x_edges.reshape(-1, N_SEG, EXTENT)
        i1, i2, i3 = (path_indices[:, 0], path_indices[:, 1], path_indices[:, 2])
        contrib = path_coeffs[None, :, None] * x1[:, i1, :] * x2[:, i2, :]
        edge_out = jnp.zeros((x2.shape[0], N_SEG, EXTENT), x_nodes.dtype).at[:, i3, :].add(contrib)
        out = jnp.zeros((n_nodes, OP_SIZE), x_nodes.dtype).at[dst].add(edge_out.reshape(-1, OP_SIZE))
        return out
    edge_index = jnp.stack([src, dst])
    h = jnp.maximum(_layernorm(x, axis=-1), 0.0)
    x = x + _L0_gnn_ref(h, edge_index, L0_gnn_W, L0_gnn_b)
    h = jnp.maximum(_layernorm(x, axis=-1), 0.0)
    x = x + _L1_gnn_ref(h, edge_attr_512, L1_gnn_path_coeffs, src, dst, L1_gnn_path_indices)
    return x

_drawn_inputs = setup_inputs


def setup_inputs(seed=0):
    import zlib

    import numpy as np

    out = dict(_drawn_inputs(seed))
    spreads = {}
    factors = {'L0_gnn_b': 7.841}
    for name, (base, spread) in spreads.items():
        noise = np.random.default_rng([zlib.crc32(name.encode()), seed]).standard_normal(out[name].shape)
        drawn = base * np.exp(spread * noise) if base else spread * noise
        out[name] = jnp.asarray(drawn.astype(out[name].dtype))
    for name, factor in factors.items():
        out[name] = (out[name] * factor).astype(out[name].dtype)
    return out
```

```python
import concourse.bass as bass
from concourse import mybir
from contextlib import ExitStack


def gnn_layers_kernel(nc, x, src, dst, edge_attr, W, bias, coeffs, paths, out):
    fp32, bf16, fp16 = mybir.dt.float32, mybir.dt.bfloat16, mybir.dt.float16
    i32, i16, u32 = mybir.dt.int32, mybir.dt.int16, mybir.dt.uint32
    ALU, ACT, AX = mybir.AluOpType, mybir.ActivationFunctionType, mybir.AxisListType
    ds = bass.ds

    P = 128
    N, D = x.shape
    E = edge_attr.shape[0]
    NP = coeffs.shape[0]
    U = 32
    EPS = 1e-5
    C = -(-N // P)
    assert C % 2 == 0
    LAST = N - (C - 1) * P
    K = D // P
    T = 15
    TI = 2 * T
    ITEMS = -(-E // (P * TI))
    FULL = E // (P * T)
    TAIL = (E - FULL * P * T) // T
    assert FULL == 2 * ITEMS - 1 and FULL * P * T + TAIL * T == E
    COLS = ITEMS * TI
    WINDOWS = N // P + 2
    G = 4
    PG = NP // G
    TURN = 2 * G
    RING = 6
    CW = C * P
    AW = CW + P
    NOWHERE = 8192
    BANK = 512

    src_full = src[0:FULL * P * T].rearrange("(b p t) -> p b t", p=P, t=T)
    dst_full = dst[0:FULL * P * T].rearrange("(b p t) -> p b t", p=P, t=T)
    src_tail = src[FULL * P * T:E].rearrange("(p t) -> p t", t=T)
    dst_tail = dst[FULL * P * T:E].rearrange("(p t) -> p t", t=T)
    edge_full = edge_attr[0:FULL * P * T, :].rearrange("(b p t) d -> p b (t d)", p=P, t=T)
    edge_tail = edge_attr[FULL * P * T:E, :].rearrange("(p t) d -> p (t d)", t=T)
    h2_dram = nc.dram_tensor("h2_rows", (N, D), fp32).ap()

    ctx = ExitStack()
    with ctx:
        def sb(name, shape, dt):
            return ctx.enter_context(nc.sbuf_tensor(name, shape, dt))

        def sem(name):
            return ctx.enter_context(nc.semaphore(name))

        x1_mem = sb("x1_mem", [P, 2 * T * D], fp32)
        x2_mem = sb("x2_mem", [P, 2 * T * D], fp32)
        q_mem = sb("q_mem", [P, 2 * T * PG * U], fp32)
        hot_mem = sb("hot_mem", [P, 2 * T * P], fp32)

        x1 = [x1_mem[:, j * T * D:(j + 1) * T * D].rearrange("p (t d) -> p t d", d=D) for j in range(2)]
        x2 = [x2_mem[:, j * T * D:(j + 1) * T * D].rearrange("p (t d) -> p t d", d=D) for j in range(2)]
        q = [q_mem[:, s * T * PG * U:(s + 1) * T * PG * U].rearrange("p (t n u) -> p t n u", n=PG, u=U)
             for s in range(2)]
        hot = [hot_mem[:, j * T * P:(j + 1) * T * P].rearrange("p (t n) -> p t n", n=P) for j in range(2)]

        class Carve:
            def __init__(self, mem):
                self.mem, self.at = mem, 0

            def take(self, words):
                self.at += words
                return self.mem[:, self.at - words:self.at]

        in_x2, in_x1, in_q, in_hot = Carve(x2_mem), Carve(x1_mem), Carve(q_mem), Carve(hot_mem)
        h1T = in_x2.take(K * CW).rearrange("p (k n) -> p k n", k=K)
        w_rows = in_x2.take(K * D).rearrange("p (k n) -> p k n", k=K)
        wT = in_x2.take(K * D).rearrange("p (k n) -> p k n", k=K)
        h1 = in_x2.take(2 * D).rearrange("p (s n) -> p s n", s=2)
        src_hot = in_x2.take(RING * CW // 2).bitcast(bf16).rearrange("p (r n) -> p r n", r=RING)
        dst_hot = in_x2.take(RING * P // 2).bitcast(bf16).rearrange("p (r n) -> p r n", r=RING)
        iota_h = in_x2.take(CW // 2).bitcast(fp16)
        ident = in_x2.take(P)

        hw = in_x1.take(C * D).rearrange("p (c n) -> p c n", c=C)
        xs = in_x1.take(C * D).rearrange("p (c n) -> p c n", c=C)
        counts = in_x1.take(CW)
        src_f = in_x1.take(COLS)
        rel0 = in_x1.take(TI)
        bias_b = in_x1.take(D)
        stats = in_x1.take(C * 6).rearrange("p (c n) -> p c n", c=C)
        mv = in_x1.take(C * 2).rearrange("p (c n) -> p c n", c=C)
        rstd = in_x1.take(C)
        shift = in_x1.take(C)
        deg = in_x1.take(C)
        dis = in_x1.take(C)
        dst_i = in_x1.take(COLS).bitcast(i32)
        span = in_x1.take(2 * ITEMS)
        span_all = in_x1.take(2 * ITEMS)
        tmp_c = in_x1.take(COLS)

        countsT = in_q.take(C * AW).rearrange("p (c n) -> p c n", c=C)

        iota_i = hot_mem[:, 0:CW].bitcast(i32)
        y = in_hot.take(2 * D).rearrange("p (s n) -> p s n", s=2)
        h2 = in_hot.take(2 * D).rearrange("p (s n) -> p s n", s=2)
        stats2 = in_hot.take(6)
        mv2 = in_hot.take(2)
        rs2 = in_hot.take(2 * 2).rearrange("p (s n) -> p s n", s=2)

        dst_f = sb("dst_f", [P, COLS], fp32)
        src_i = sb("src_i", [P, COLS], i32)
        src_now = sb("src_now", [P, 2, T], i32)
        iota_f = sb("iota_f", [P, P], fp32)
        base_f = sb("base_f", [P, ITEMS], fp32)
        bases = sb("bases", [P, ITEMS, WINDOWS], fp32)
        meta = sb("meta", [P, 2 * ITEMS], i32)
        coef = sb("coef", [P, NP], fp32)
        path_i = sb("path_i", [1, NP * 3], i32)
        i12 = sb("i12", [1, NP, 2], i16)
        i3 = sb("i3", [1, NP], i16)
        rel1 = sb("rel1", [P, 2, T], fp32)
        S = sb("S", [P, 2, PG * U], fp32)
        acc = sb("acc", [P, D], fp32)

        ps = [ctx.enter_context(nc.psum_tensor(f"ps{i}", [P, BANK], fp32)) for i in range(8)]

        x_in, idx_in, w_in, small_in = sem("x_in"), sem("idx_in"), sem("w_in"), sem("small_in")
        pads_set, iota_done, ident_done = sem("pads_set"), sem("iota_done"), sem("ident_done")
        consts_ready, zeros_set, countsT_init = sem("consts_ready"), sem("zeros_set"), sem("countsT_init")
        span_ready, span_reduced, meta_ready = sem("span_ready"), sem("span_reduced"), sem("meta_ready")
        v_chain, a_chain, g_chain = sem("v_chain"), sem("a_chain"), sem("g_chain")
        var_ready, root_ready = sem("var_ready"), sem("root_ready")
        norm_ready, h1_ready, h1_transposed = sem("norm_ready"), sem("h1_ready"), sem("h1_transposed")
        h1T_ready, w_transposed, wT_ready = sem("h1T_ready"), sem("w_transposed"), sem("wT_ready")
        hw_summed, hw_ready = sem("hw_summed"), sem("hw_ready")
        hots_ready, hots_used = sem("hots_ready"), sem("hots_used")
        counts_saved = sem("counts_saved")
        counts_transposed, counts_added = sem("counts_transposed"), sem("counts_added")
        g_ready, agg_summed, y_ready = sem("g_ready"), sem("agg_summed"), sem("y_ready")
        xs_ready, h2_ready = sem("xs_ready"), sem("h2_ready")
        h2_stored = [sem(f"h2_stored{i}") for i in range(2)]
        xs_stored = sem("xs_stored")
        x1_in = [sem(f"x1_in{j}") for j in range(2)]
        x2_in = [sem(f"x2_in{j}") for j in range(2)]
        multiplied, summed = sem("multiplied"), sem("summed")
        hot_ready, saved, s_free = sem("hot_ready"), sem("saved"), sem("s_free")
        idx_copied, out_added = sem("idx_copied"), sem("out_added")
        mixed = sem("mixed")
        pool_steps = sem("pool_steps")

        def group(turn, s):
            return turn * TURN + TURN + s + 1

        def group_before(turn, s):
            return turn * TURN + s + 1

        def turns(eng, first, body):
            with eng.Fori(0, ITEMS) as item:
                one_item(eng, item, first, body)

        def one_item(eng, item, count, body):
            base = eng.value_load(meta[0:1, ds(item, 1)], min_val=0, max_val=N - 1)
            far = eng.value_load(meta[0:1, ds(item + ITEMS, 1)], min_val=0, max_val=N - 1)
            with eng.Fori(0, (far >> 7) + 1) as window:
                turn = eng.snap(count, min_val=0, max_val=ITEMS * WINDOWS - 1)
                body(item, window, turn, base)
                eng.reg_add(count, count, 1)

        def counter(eng, name):
            r = eng.alloc_register(name)
            eng.reg_mov(r, 0)
            return r

        block = ctx.enter_context(nc.Block())

        @block.sync
        def _(sp):
            sp.wait_ge(pads_set, 3)
            sp.dma_start(xs[:, 0:C - 1, :], x[0:(C - 1) * P, :].rearrange("(c p) d -> p c d", p=P)).then_inc(x_in, 16)
            sp.dma_start(xs[0:LAST, C - 1, :], x[(C - 1) * P:N, :]).then_inc(x_in, 16)
            sp.dma_start(w_rows, W.rearrange("(k p) d -> p k d", p=P)).then_inc(w_in, 16)
            sp.dma_start(bias_b, bias.rearrange("(a n) -> a n", a=1).broadcast_to([P, D])).then_inc(small_in, 16)
            sp.dma_start(coef[:, :], coeffs.rearrange("(a n) -> a n", a=1).broadcast_to([P, NP])).then_inc(small_in, 16)
            sp.dma_start(path_i[:, :], paths.rearrange("(a n) c -> a (n c)", a=1)).then_inc(small_in, 16)

            sp.wait_ge(meta_ready, 1)
            turn_count = counter(sp, "sp_turn")

            def load(j, turn, tail, b):
                sp.wait_ge(multiplied, group_before(turn, j * G + G - 1))
                if tail:
                    sp.dma_start(x2_mem[0:TAIL, j * T * D:(j + 1) * T * D], edge_tail).then_inc(x2_in[j], 16)
                else:
                    sp.dma_start(x2_mem[:, j * T * D:(j + 1) * T * D], edge_full[:, ds(b, 1), :].rearrange("p b n -> p (b n)")).then_inc(x2_in[j], 16)

            def body(item, window, turn, base):
                for j in range(2):
                    load(j, turn, False, item * 2 + j)

            def body_last(item, window, turn, base):
                load(0, turn, False, item * 2)
                load(1, turn, True, None)

            sp.wait_ge(g_ready, 1)
            with sp.Fori(0, ITEMS - 1) as item:
                one_item(sp, item, turn_count, body)
            one_item(sp, ITEMS - 1, turn_count, body_last)

        @block.gpsimd
        def _(pool):
            nc.gpsimd.memset(xs[96:P, C - 1, :], 0.0).then_inc(pads_set, 1)
            pool.wait_ge(pads_set, 1)
            nc.gpsimd.memset(dst_i, NOWHERE).then_inc(pads_set, 1)
            nc.gpsimd.memset(src_i[:, :], 0).then_inc(pads_set, 1)
            nc.gpsimd.iota(iota_i, pattern=[[1, CW]], base=0, channel_multiplier=0).then_inc(iota_done, 1)
            nc.gpsimd.memset(ident, 0.0).then_inc(g_chain, 1)
            pool.wait_ge(g_chain, 1)
            nc.gpsimd.affine_select(out=ident, in_=ident, compare_op=ALU.not_equal, fill=1.0, base=0,
                                    pattern=[[-1, P]], channel_multiplier=1).then_inc(ident_done, 1)
            nc.gpsimd.memset(acc[:, :], 0.0).then_inc(zeros_set, 1)
            nc.gpsimd.memset(counts, 0.0).then_inc(zeros_set, 1)
            pool.wait_ge(span_ready, 1)
            nc.gpsimd.partition_all_reduce(span_all, span, P, bass.bass_isa.ReduceOp.max).then_inc(span_reduced, 1)
            nc.gpsimd.memset(countsT, 0.0).then_inc(g_chain, 1)
            pool.wait_ge(g_chain, 2)
            pool.wait_ge(ident_done, 1)
            for c in range(C):
                nc.gpsimd.tensor_copy(countsT[:, c, c * P:(c + 1) * P], ident).then_inc(countsT_init, 1)
            pool.wait_ge(zeros_set, 1)
            pool.dma_start(out[N:N + P, :], acc[:, :]).then_inc(out_added, 16)

            pool.wait_ge(meta_ready, 1)
            for i in range(2):
                pool.wait_ge(h2_stored[i], 16 * (C // 2))
            pool.wait_ge(xs_stored, 16 * C)
            pool.wait_ge(out_added, 16)
            pool.wait_ge(summed, TURN)
            pool.sem_inc(s_free, 2)
            turn_count = counter(pool, "pool_turn")
            row_reg = counter(pool, "pool_row")
            i3_regs = [pool.alloc_register(f"i3_{n}") for n in range(PG)]

            def mix(turn):
                pool.wait_ge(out_added, turn * 16 + 16)
                pool.sem_inc(pool_steps, 1)
                pool.sem_clear(mixed)
                nc.gpsimd.memset(acc[:, :], 0.0).then_inc(mixed, 1)
                for g in range(G):
                    pool.load(i3_regs, i3[0:1, g * PG:(g + 1) * PG])
                    pool.wait_ge(saved, turn * G + g + 1)
                    pool.sem_inc(pool_steps, 1)
                    for n in range(PG):
                        to = pool.snap(i3_regs[n], min_val=0, max_val=D - U)
                        pool.wait_ge(mixed, g * PG + n + 1)
                        nc.gpsimd.tensor_tensor(acc[:, ds(to, U)], acc[:, ds(to, U)],
                                                S[:, g % 2, n * U:(n + 1) * U], ALU.add).then_inc(mixed, 1)
                    pool.wait_ge(mixed, g * PG + PG + 1)
                    pool.sem_inc(s_free, 1)
                row = pool.snap(row_reg, min_val=0, max_val=N - 1)
                pool.dma_start(out[ds(row, P), :], acc[:, :], accum_op=ALU.add).then_inc(out_added, 16)

            def body(item, window, turn, base):
                for j in range(2):
                    pool.wait_ge(multiplied, group_before(turn, j * G + G - 1))
                    nc.gpsimd.tensor_copy(src_now[:, j, :], src_i[:, ds((item * 2 + j) * T, T)]).then_inc(idx_copied, 1)
                    pool.wait_ge(idx_copied, turn * 2 + j + 1)
                    pool.sem_inc(pool_steps, 1)
                    for t in range(T):
                        pool.indirect_dma_start(x1[j][:, t, :], None, h2_dram[:, :],
                                                bass.IndirectOffsetOnAxis(ap=src_now[:, j, t:t + 1].bitcast(u32), axis=0)
                                                ).then_inc(x1_in[j], 16)
                mix(turn)
                pool.reg_mov(row_reg, base + window * P)

            turns(pool, turn_count, body)
            mix(pool.snap(turn_count, min_val=1, max_val=ITEMS * WINDOWS))
            pool.wait_ge(out_added, pool.snap(turn_count, min_val=1, max_val=ITEMS * WINDOWS) * 16 + 32)

        @block.vector
        def _(dve):
            chain = [0]

            def link(ins):
                chain[0] += 1
                ins.then_inc(v_chain, 1)
                dve.wait_ge(v_chain, chain[0])

            dve.wait_ge(iota_done, 1)
            nc.vector.tensor_copy(iota_h, iota_i).then_inc(consts_ready, 1)
            nc.vector.tensor_copy(iota_f[:, :], iota_i[:, 0:P]).then_inc(consts_ready, 1)

            dve.wait_ge(idx_in, 64)
            nc.vector.tensor_copy(src_f, src_i[:, :])
            link(nc.vector.tensor_copy(dst_f[:, :], dst_i))
            link(nc.vector.tensor_scalar(tmp_c, dst_f[:, :], -1.0, None, ALU.mult))
            nc.vector.tensor_reduce(span[:, 0:ITEMS], tmp_c.rearrange("p (i t) -> p i t", t=TI), AX.X, ALU.max)
            link(nc.vector.tensor_scalar(dst_i.bitcast(fp32), dst_f[:, :], float(NOWHERE), None, ALU.is_lt))
            link(nc.vector.tensor_tensor(tmp_c, dst_i.bitcast(fp32), dst_f[:, :], ALU.mult))
            nc.vector.tensor_reduce(span[:, ITEMS:2 * ITEMS], tmp_c.rearrange("p (i t) -> p i t", t=TI), AX.X,
                                    ALU.max).then_inc(span_ready, 1)
            dve.wait_ge(span_reduced, 1)
            link(nc.vector.tensor_scalar(base_f[:, :], span_all[:, 0:ITEMS], -1.0, None, ALU.mult))
            for k in range(WINDOWS):
                nc.vector.tensor_scalar(bases[:, :, k], base_f[:, :], float(k * P), None, ALU.add)
            link(nc.vector.tensor_tensor(tmp_c[:, 0:ITEMS], span_all[:, ITEMS:2 * ITEMS], base_f[:, :], ALU.subtract))
            link(nc.vector.tensor_copy(meta[:, 0:ITEMS], base_f[:, :]))
            nc.vector.tensor_copy(meta[:, ITEMS:2 * ITEMS], tmp_c[:, 0:ITEMS]).then_inc(meta_ready, 1)

            dve.wait_ge(x_in, 32)
            for c in range(C):
                last = nc.vector.bn_stats(stats[:, c, :], xs[:, c, :])
            link(last)
            for c in range(C):
                last = nc.vector.bn_aggr(mv[:, c, :], stats[:, c, :])
            link(last)
            nc.vector.tensor_scalar(rstd, mv[:, :, 1], EPS, None, ALU.add).then_inc(var_ready, 1)
            dve.wait_ge(root_ready, 1)
            link(nc.vector.reciprocal(rstd, rstd))
            link(nc.vector.tensor_tensor(shift, mv[:, :, 0], rstd, ALU.mult))
            nc.vector.tensor_scalar(shift, shift, -1.0, None, ALU.mult).then_inc(norm_ready, 1)

            dve.wait_ge(small_in, 48)
            pv = path_i[:, :].rearrange("a (n c) -> a n c", c=3)
            nc.vector.tensor_scalar(i12[:, :, :], pv[:, :, 0:2], U, None, ALU.mult)
            link(nc.vector.tensor_scalar(i3[:, :], pv[:, :, 2], U, None, ALU.mult))

            for k in range(K):
                dve.wait_ge(w_transposed, k + 1)
                nc.vector.tensor_copy(wT[:, k, :], ps[2 + k % 2][:, :]).then_inc(wT_ready, 1)
            for c in range(C + 1):
                if c < C:
                    dve.wait_ge(h1_transposed, c + 1)
                    nc.vector.tensor_copy(h1T[:, :, c * P:(c + 1) * P],
                                          ps[c % 2][:, :].rearrange("p (k n) -> p k n", k=K)).then_inc(h1T_ready, 1)
                if c:
                    dve.wait_ge(hw_summed, c)
                    nc.vector.tensor_tensor(hw[:, c - 1, :], ps[4 + (c - 1) % 2][:, :], bias_b, ALU.add).then_inc(hw_ready, 1)

            dve.wait_ge(consts_ready, 2)
            dve.wait_ge(countsT_init, C)
            turn_count = counter(dve, "dve_turn0")
            row_reg = counter(dve, "dve_row")
            dve.sem_inc(hots_ready, 1)
            chained = chain[0]

            def add_counts(turn):
                dve.wait_ge(counts_transposed, turn + 1)
                row = dve.snap(row_reg, min_val=0, max_val=N - 1)
                for b in range(3):
                    n = min(4, C - 4 * b)
                    to = countsT[:, 4 * b:4 * b + n, ds(row, P)]
                    last = nc.vector.tensor_tensor(to, ps[3 + b][:, 0:n * P].rearrange("p (c n) -> p c n", n=P), to, ALU.add)
                last.then_inc(counts_added, 1)

            def count_body(item, window, turn, base):
                dve.wait_ge(hots_ready, turn * TI + 1)
                nc.vector.tensor_scalar(rel0, dst_f[:, ds(item * TI, TI)],
                                        bases[:, ds(item, 1), ds(window, 1)].rearrange("p a b -> p (a b)"),
                                        None, ALU.subtract).then_inc(v_chain, 1)
                dve.wait_ge(v_chain, turn + (chained + 1))
                for t in range(TI):
                    dve.wait_ge(hots_used, turn * TI + (t + 1))
                    nc.vector.tensor_scalar(dst_hot[:, t % RING, :], iota_h[:, 0:P], rel0[:, t:t + 1], None, ALU.is_equal)
                    nc.vector.tensor_scalar(src_hot[:, t % RING, :], iota_h, src_f[:, ds(item * TI + t, 1)], None,
                                            ALU.is_equal).then_inc(hots_ready, 1)
                    if t == RING:
                        add_counts(turn)
                dve.reg_mov(row_reg, base + window * P)

            turns(dve, turn_count, count_body)
            add_counts(dve.snap(turn_count, min_val=1, max_val=ITEMS * WINDOWS))

            dve.wait_ge(counts_added, dve.snap(turn_count, min_val=1, max_val=ITEMS * WINDOWS) + 2)
            dve.wait_ge(hw_ready, C)
            nc.vector.tensor_reduce(deg, countsT, AX.X, ALU.add).then_inc(g_ready, 1)
            dve.wait_ge(g_ready, 1)
            nc.vector.tensor_scalar(dis, deg, 1.0, None, ALU.mult).then_inc(var_ready, 1)
            dve.wait_ge(root_ready, 2)
            nc.vector.reciprocal(dis, dis).then_inc(g_ready, 1)
            dve.wait_ge(g_ready, 2)
            for c in range(C):
                nc.vector.tensor_scalar(hw[:, c, :], hw[:, c, :], dis[:, c:c + 1], None, ALU.mult).then_inc(g_ready, 1)

            for c in range(C):
                dve.wait_ge(y_ready, c + 1)
                nc.vector.tensor_tensor(xs[:, c, :], xs[:, c, :], y[:, c % 2, :], ALU.add).then_inc(xs_ready, 1)
                dve.wait_ge(xs_ready, 5 * c + 1)
                nc.vector.bn_stats(stats2, xs[:, c, :]).then_inc(xs_ready, 1)
                dve.wait_ge(xs_ready, 5 * c + 2)
                nc.vector.bn_aggr(mv2, stats2).then_inc(xs_ready, 1)
                dve.wait_ge(xs_ready, 5 * c + 3)
                if c >= 2:
                    dve.wait_ge(h2_ready, c - 1)
                nc.vector.tensor_scalar(rs2[:, c % 2, 0:1], mv2[:, 1:2], EPS, None, ALU.add).then_inc(var_ready, 1)
                dve.wait_ge(root_ready, c + 3)
                nc.vector.reciprocal(rs2[:, c % 2, 0:1], rs2[:, c % 2, 0:1]).then_inc(xs_ready, 1)
                dve.wait_ge(xs_ready, 5 * c + 4)
                nc.vector.tensor_scalar(rs2[:, c % 2, 1:2], mv2[:, 0:1], rs2[:, c % 2, 0:1], -1.0, ALU.mult,
                                        ALU.mult).then_inc(xs_ready, 1)

            dve.sem_inc(multiplied, TURN)
            turn_count = counter(dve, "dve_turn1")
            regs = [dve.alloc_register(f"i12_{n}") for n in range(PG)]

            def product_body(item, window, turn, base):
                for j in range(2):
                    for g in range(G):
                        s = j * G + g
                        for half in range(2):
                            p0 = g * PG + half * (PG // 2)
                            dve.load(regs, i12[0:1, p0:p0 + PG // 2, :].rearrange("a n c -> a (n c)"))
                            if g == 0 and half == 0:
                                dve.wait_ge(x1_in[j], turn * (16 * T) + 16 * T)
                                dve.wait_ge(x2_in[j], turn * 16 + 16)
                            if half == 0:
                                dve.wait_ge(summed, group(turn, s - 2))
                            for n in range(PG // 2):
                                a = dve.snap(regs[2 * n], min_val=0, max_val=D - U)
                                b = dve.snap(regs[2 * n + 1], min_val=0, max_val=D - U)
                                last = nc.vector.scalar_tensor_tensor(
                                    out=q[s % 2][:, :, half * (PG // 2) + n, :], in0=x1[j][:, :, ds(a, U)],
                                    scalar=coef[:, p0 + n:p0 + n + 1], in1=x2[j][:, :, ds(b, U)],
                                    op0=ALU.mult, op1=ALU.mult)
                        last.then_inc(multiplied, 1)

            turns(dve, turn_count, product_body)

        @block.scalar
        def _(act):
            act.wait_ge(pads_set, 3)
            act.dma_start(src_i[:, 0:FULL * T].rearrange("p (b t) -> p b t", t=T), src_full).then_inc(idx_in, 16)
            act.dma_start(dst_i[:, 0:FULL * T].rearrange("p (b t) -> p b t", t=T), dst_full).then_inc(idx_in, 16)
            act.dma_start(src_i[0:TAIL, FULL * T:COLS], src_tail).then_inc(idx_in, 16)
            act.dma_start(dst_i[0:TAIL, FULL * T:COLS], dst_tail).then_inc(idx_in, 16)

            act.wait_ge(x_in, 32)
            act.wait_ge(var_ready, 1)
            nc.scalar.activation(rstd, rstd, ACT.Sqrt).then_inc(root_ready, 1)
            act.wait_ge(norm_ready, 1)
            for c in range(C):
                if c >= 2:
                    act.wait_ge(h1_transposed, c - 1)
                nc.scalar.activation(h1[:, c % 2, :], xs[:, c, :], ACT.Relu, bias=shift[:, c:c + 1],
                                     scale=rstd[:, c:c + 1]).then_inc(h1_ready, 1)

            act.wait_ge(meta_ready, 1)
            act.wait_ge(zeros_set, 2)
            act.sem_inc(counts_saved, 3)
            turn_count = counter(act, "act_turn0")

            def save_body(item, window, turn, base):
                act.wait_ge(counts_transposed, turn + 1)
                act.wait_ge(hots_used, turn * TI + (RING + TI))
                for b in range(3):
                    n = min(BANK, N - BANK * b)
                    nc.scalar.activation(counts[:, BANK * b:BANK * b + n], ps[b][:, 0:n], ACT.Copy).then_inc(counts_saved, 1)

            turns(act, turn_count, save_body)

            act.wait_ge(var_ready, 2)
            nc.scalar.activation(dis, dis, ACT.Sqrt).then_inc(root_ready, 1)
            act.wait_ge(g_ready, 2 + C)
            for c in range(C):
                rows = P if c < C - 1 else LAST
                act.wait_ge(agg_summed, c + 1)
                nc.scalar.activation(y[:, c % 2, :], ps[6 + c % 2][:, :], ACT.Relu, scale=dis[:, c:c + 1]).then_inc(y_ready, 1)
                act.wait_ge(var_ready, c + 3)
                nc.scalar.activation(rs2[:, c % 2, 0:1], rs2[:, c % 2, 0:1], ACT.Sqrt).then_inc(root_ready, 1)
                act.wait_ge(xs_ready, 5 * c + 5)
                if c >= 2:
                    act.wait_ge(h2_stored[c % 2], 16 * (c // 2))
                nc.scalar.activation(h2[:, c % 2, :], xs[:, c, :], ACT.Relu, bias=rs2[:, c % 2, 1:2],
                                     scale=rs2[:, c % 2, 0:1]).then_inc(h2_ready, 1)
                act.dma_start(out[c * P:c * P + rows, :], xs[0:rows, c, :]).then_inc(xs_stored, 16)
                act.wait_ge(h2_ready, c + 1)
                act.dma_start(h2_dram[c * P:c * P + rows, :], h2[0:rows, c % 2, :]).then_inc(h2_stored[c % 2], 16)
            for i in range(2):
                act.wait_ge(h2_stored[i], 16 * (C // 2))

            turn_count = counter(act, "act_turn1")

            def one_hots(j, item, window, turn):
                act.wait_ge(summed, group_before(turn, j * G + G - 1))
                nc.scalar.activation(rel1[:, j, :], dst_f[:, ds((item * 2 + j) * T, T)], ACT.Identity, scale=-1.0,
                                     bias=bases[:, ds(item, 1), ds(window, 1)].rearrange("p a b -> p (a b)")).then_inc(a_chain, 1)
                act.wait_ge(a_chain, turn * 4 + 2 * j + 1)
                for t in range(T):
                    last = nc.scalar.activation(hot[j][:, t, :], iota_f[:, :], ACT.Abs, bias=rel1[:, j, t:t + 1])
                last.then_inc(a_chain, 1)
                act.wait_ge(a_chain, turn * 4 + 2 * j + 2)
                nc.scalar.activation(hot[j], hot[j], ACT.Relu, scale=-1.0, bias=1.0).then_inc(hot_ready, 1)

            def save(turn):
                for g in range(G):
                    act.wait_ge(summed, group_before(turn, G + g))
                    act.wait_ge(s_free, turn * G + g + 1)
                    nc.scalar.activation(S[:, g % 2, :], ps[g][:, :], ACT.Copy).then_inc(saved, 1)

            def act_body(item, window, turn, base):
                one_hots(0, item, window, turn)
                save(turn)
                one_hots(1, item, window, turn)

            turns(act, turn_count, act_body)
            save(act.snap(turn_count, min_val=1, max_val=ITEMS * WINDOWS))

        @block.tensor
        def _(pe):
            pe.wait_ge(ident_done, 1)
            pe.wait_ge(w_in, 16)
            for k in range(K):
                if k >= 2:
                    pe.wait_ge(wT_ready, k - 1)
                for o in range(K):
                    last = nc.tensor.transpose(ps[2 + k % 2][:, o * P:(o + 1) * P], w_rows[:, o, k * P:(k + 1) * P], ident)
                last.then_inc(w_transposed, 1)
            pe.wait_ge(wT_ready, K)
            for c in range(C + 1):
                if c < C:
                    pe.wait_ge(h1_ready, c + 1)
                    if c >= 2:
                        pe.wait_ge(h1T_ready, c - 1)
                    for k in range(K):
                        last = nc.tensor.transpose(ps[c % 2][:, k * P:(k + 1) * P], h1[:, c % 2, k * P:(k + 1) * P], ident)
                    last.then_inc(h1_transposed, 1)
                if c:
                    e = c - 1
                    pe.wait_ge(h1T_ready, c)
                    if e >= 2:
                        pe.wait_ge(hw_ready, e - 1)
                    for k in range(K):
                        last = nc.tensor.matmul(ps[4 + e % 2][:, :], h1T[:, k, e * P:(e + 1) * P], wT[:, k, :],
                                                start=(k == 0), stop=(k == K - 1))
                    last.then_inc(hw_summed, 1)

            pe.wait_ge(meta_ready, 1)
            pe.wait_ge(hw_ready, C)
            pe.wait_ge(zeros_set, 2)
            pe.sem_inc(hots_used, RING)
            pe.sem_inc(counts_added, 1)
            turn_count = counter(pe, "pe_turn0")

            def transpose_counts(turn):
                pe.wait_ge(counts_added, turn + 1)
                for c in range(C):
                    last = nc.tensor.transpose(ps[3 + c // 4][:, (c % 4) * P:(c % 4 + 1) * P],
                                               counts[:, c * P:(c + 1) * P], ident)
                last.then_inc(counts_transposed, 1)

            def count_body(item, window, turn, base):
                pe.wait_ge(counts_saved, turn * 3 + 3)
                for t in range(TI):
                    pe.wait_ge(hots_ready, turn * TI + (t + 2))
                    for b in range(3):
                        n = min(BANK, N - BANK * b)
                        last = nc.tensor.matmul(ps[b][:, 0:n], dst_hot[:, t % RING, :],
                                                src_hot[:, t % RING, BANK * b:BANK * b + n],
                                                start=(t == 0), stop=(t == TI - 1))
                    last.then_inc(hots_used, 1)
                    if t == RING - 1:
                        transpose_counts(turn)

            turns(pe, turn_count, count_body)
            pe.wait_ge(counts_saved, pe.snap(turn_count, min_val=1, max_val=ITEMS * WINDOWS) * 3 + 3)
            transpose_counts(pe.snap(turn_count, min_val=1, max_val=ITEMS * WINDOWS))

            pe.wait_ge(g_ready, 2 + C)
            for c in range(C):
                if c >= 2:
                    pe.wait_ge(y_ready, c - 1)
                for m in range(C):
                    last = nc.tensor.matmul(ps[6 + c % 2][:, :], countsT[:, m, c * P:(c + 1) * P], hw[:, m, :],
                                            start=(m == 0), stop=(m == C - 1))
                last.then_inc(agg_summed, 1)

            turn_count = counter(pe, "pe_turn1")
            pe.wait_ge(zeros_set, 1)
            for g in range(G):
                last = nc.tensor.matmul(ps[g][:, :], acc[:, 0:P], acc[:, :], start=True, stop=True)
            last.then_inc(summed, TURN)

            def sum_body(item, window, turn, base):
                for j in range(2):
                    pe.wait_ge(hot_ready, turn * 2 + j + 1)
                    for g in range(G):
                        s = j * G + g
                        pe.wait_ge(multiplied, group(turn, s))
                        if j == 0:
                            pe.wait_ge(saved, turn * G + g + 1)
                        for t in range(T):
                            last = nc.tensor.matmul(ps[g][:, :], hot[j][:, t, :],
                                                    q[s % 2][:, t, :, :].rearrange("p n u -> p (n u)"),
                                                    start=(j == 0 and t == 0), stop=(j == 1 and t == T - 1))
                        last.then_inc(summed, 1)

            turns(pe, turn_count, sum_body)


_INS = ["x", "src", "dst", "edge_attr_512", "L0_gnn_W", "L0_gnn_b", "L1_gnn_path_coeffs", "L1_gnn_path_indices"]


def kernel(**inputs):
    import numpy as _np
    import concourse.bacc as _bacc
    from concourse import mybir as _mybir
    from concourse.bass_utils import run_bass_kernel_spmd as _run

    nc = _bacc.Bacc("TRN2", target_bir_lowering=False, num_devices=1)
    arrays, args = {}, []
    for name in _INS:
        a = _np.ascontiguousarray(inputs[name])
        arrays[f"in_{name}"] = a
        args.append(nc.dram_tensor(f"in_{name}", a.shape, _mybir.dt.from_np(a.dtype), kind="ExternalInput").ap())
    n, d = arrays["in_x"].shape
    args.append(nc.dram_tensor("out_0", (n + 128, d), _mybir.dt.float32, kind="ExternalOutput").ap())
    gnn_layers_kernel(nc, *args)
    r = _run(nc, [arrays], core_ids=[0])
    return r.results[0]["out_0"][:n]
```

```python
import concourse.bass as bass
from concourse import mybir
from contextlib import ExitStack


def gnn_layers_kernel(nc, x, src, dst, edge_attr, W, bias, coeffs, paths, out):
    fp32, bf16, fp16 = mybir.dt.float32, mybir.dt.bfloat16, mybir.dt.float16
    i32, i16, u32 = mybir.dt.int32, mybir.dt.int16, mybir.dt.uint32
    ALU, ACT, AX = mybir.AluOpType, mybir.ActivationFunctionType, mybir.AxisListType
    ds = bass.ds

    P = 128
    N, D = x.shape
    E = edge_attr.shape[0]
    NP = coeffs.shape[0]
    U = 32
    EPS = 1e-5
    C = -(-N // P)
    assert C % 2 == 0
    LAST = N - (C - 1) * P
    K = D // P
    T = 15
    TB = [8, 7]
    T0 = [0, 8]
    TI = 2 * T
    M = P // 2
    ITEMS = -(-E // (P * TI))
    FULL = E // (P * T)
    TAIL = (E - FULL * P * T) // T
    assert FULL == 2 * ITEMS - 1 and FULL * P * T + TAIL * T == E
    SIDES = 2 * ITEMS
    COLS = ITEMS * TI
    WINDOWS = N // M + 2
    G = 4
    PG = NP // G
    TURN = 2 * G
    QT = 2 * TB[0]
    RING = 15
    CW = C * P
    AW = CW + M
    NOWHERE = 8192
    BANK = 512

    src_full = src[0:FULL * P * T].rearrange("(b p t) -> p b t", p=P, t=T)
    dst_full = dst[0:FULL * P * T].rearrange("(b p t) -> p b t", p=P, t=T)
    src_tail = src[FULL * P * T:E].rearrange("(p t) -> p t", t=T)
    dst_tail = dst[FULL * P * T:E].rearrange("(p t) -> p t", t=T)
    edge_full = edge_attr[0:FULL * P * T, :].rearrange("(b p t) d -> p b (t d)", p=P, t=T)
    edge_tail = edge_attr[FULL * P * T:E, :].rearrange("(p t) d -> p (t d)", t=T)
    h2_dram = nc.dram_tensor("h2_rows", (N, D), fp32).ap()

    ctx = ExitStack()
    with ctx:
        def sb(name, shape, dt):
            return ctx.enter_context(nc.sbuf_tensor(name, shape, dt))

        def sem(name):
            return ctx.enter_context(nc.semaphore(name))

        x1_mem = sb("x1_mem", [P, TI * D], fp32)
        x2_mem = sb("x2_mem", [P, TI * D], fp32)
        q_mem = sb("q_mem", [P, 2 * QT * PG * U], fp32)
        hot_mem = sb("hot_mem", [P, TI * M], fp32)

        def batch(mem, j):
            at, n = 2 * T0[j] * D, 2 * TB[j] * D
            return mem[:, at:at + n]

        x1 = [batch(x1_mem, j).rearrange("p (t d) -> p t d", d=D) for j in range(2)]
        x2 = [batch(x2_mem, j).rearrange("p (t d) -> p t d", d=D) for j in range(2)]
        q = [q_mem[:, s * QT * PG * U:(s + 1) * QT * PG * U].rearrange("p (t n u) -> p t n u", n=PG, u=U)
             for s in range(2)]
        hot = [hot_mem[:, 2 * T0[j] * M:2 * (T0[j] + TB[j]) * M].rearrange("p (s t n) -> p s t n", s=2, n=M)
               for j in range(2)]

        class Carve:
            def __init__(self, mem):
                self.mem, self.at = mem, 0

            def take(self, words):
                self.at += words
                return self.mem[:, self.at - words:self.at]

        in_x2, in_x1, in_q = Carve(x2_mem), Carve(x1_mem), Carve(q_mem)
        w_rows = in_x2.take(K * D).rearrange("p (k n) -> p k n", k=K)
        wT = in_x2.take(K * D).rearrange("p (k n) -> p k n", k=K)
        h1 = in_x2.take(D)
        h1T = in_x2.take(D)
        src_hot = in_x2.take(RING * CW // 2).bitcast(bf16).rearrange("p (r n) -> p r n", r=RING)
        iota_h = in_x2.take(CW // 2).bitcast(fp16)
        dst_hot = [hot_mem[:, T0[j] * M:(T0[j] + TB[j]) * M].bitcast(bf16).rearrange("p (t n) -> p t n", n=M)
                   for j in range(2)]

        hw = in_x1.take((C + 1) * D).rearrange("p (c n) -> p c n", c=C + 1)
        xs = in_x1.take(C * D).rearrange("p (c n) -> p c n", c=C)
        counts = in_x1.take(CW)
        src_f = in_x1.take(COLS)
        rel0 = in_x1.take(2 * TI)
        stats = in_x1.take(C * 6).rearrange("p (c n) -> p c n", c=C)
        mv = in_x1.take(C * 2).rearrange("p (c n) -> p c n", c=C)
        rstd = in_x1.take(C)
        shift = in_x1.take(C)
        deg = in_x1.take(C)
        dis = in_x1.take(C)
        y = in_x1.take(2 * D).rearrange("p (s n) -> p s n", s=2)
        h2 = in_x1.take(2 * D).rearrange("p (s n) -> p s n", s=2)
        stats2 = in_x1.take(6)
        mv2 = in_x1.take(2)
        rs2 = in_x1.take(2 * 2).rearrange("p (s n) -> p s n", s=2)

        countsT = in_q.take(C * AW).rearrange("p (c n) -> p c n", c=C)
        iota_i = in_q.take(CW).bitcast(i32)
        ident = in_q.take(P)
        dst_i = in_q.take(COLS).bitcast(i32)
        tmp_c = in_q.take(COLS)
        span = in_q.take(2 * SIDES)
        span_all = in_q.take(2 * SIDES)
        first_row = in_q.take(P)
        bias_b = in_q.take(D)

        dst_f = sb("dst_f", [P, COLS], fp32)
        src_i = sb("src_i", [P, COLS], i32)
        src_now = sb("src_now", [P, TI], i32)
        iota_f = sb("iota_f", [P, M], fp32)
        shift_w = sb("shift_w", [P, WINDOWS], fp32)
        base_f = sb("base_f", [P, SIDES], fp32)
        meta = sb("meta", [P, SIDES + ITEMS], i32)
        coef = sb("coef", [P, NP], fp32)
        path_i = sb("path_i", [1, NP * 3], i32)
        i12 = sb("i12", [1, NP, 2], i16)
        i3 = sb("i3", [1, NP], i16)
        rel = sb("rel", [P, 2, TI], fp32)
        S = sb("S", [P, 2, PG * U], fp32)
        acc = sb("acc", [P, D], fp32)

        psum = ctx.enter_context(nc.psum_tensor("psum", [P, 8 * BANK], fp32))
        ps = [psum[:, i * BANK:(i + 1) * BANK] for i in range(8)]
        psT = psum[:, 3 * BANK:3 * BANK + CW].rearrange("p (c n) -> p c n", n=P)

        x_in, idx_in, w_in, small_in = sem("x_in"), sem("idx_in"), sem("w_in"), sem("small_in")
        pads_set, iota_done, ident_done = sem("pads_set"), sem("iota_done"), sem("ident_done")
        consts_ready, zeros_set, countsT_init = sem("consts_ready"), sem("zeros_set"), sem("countsT_init")
        span_ready, span_reduced, meta_ready = sem("span_ready"), sem("span_reduced"), sem("meta_ready")
        v_chain, a_chain0, a_chain1, g_chain = sem("v_chain"), sem("a_chain0"), sem("a_chain1"), sem("g_chain")
        var_ready, root_ready = sem("var_ready"), sem("root_ready")
        norm_ready, h1_ready, h1_transposed = sem("norm_ready"), sem("h1_ready"), sem("h1_transposed")
        h1T_ready, w_transposed, wT_ready = sem("h1T_ready"), sem("w_transposed"), sem("wT_ready")
        hw_summed, hw_saved, dst_ready = sem("hw_summed"), sem("hw_saved"), sem("dst_ready")
        hots_ready, hots_used = sem("hots_ready"), sem("hots_used")
        counts_saved = sem("counts_saved")
        counts_transposed, counts_added = sem("counts_transposed"), sem("counts_added")
        g_ready, agg_summed, y_ready = sem("g_ready"), sem("agg_summed"), sem("y_ready")
        xs_ready, h2_ready = sem("xs_ready"), sem("h2_ready")
        h2_stored = [sem(f"h2_stored{i}") for i in range(2)]
        xs_stored = sem("xs_stored")
        x1_in = [sem(f"x1_in{j}") for j in range(2)]
        x2_in = [sem(f"x2_in{j}") for j in range(2)]
        multiplied, summed = sem("multiplied"), sem("summed")
        hot_ready, saved, s_free = sem("hot_ready"), sem("saved"), sem("s_free")
        idx_copied, out_added = sem("idx_copied"), sem("out_added")
        mixed = sem("mixed")
        pool_steps = sem("pool_steps")

        def group(turn, s):
            return turn * TURN + TURN + s + 1

        def group_before(turn, s):
            return turn * TURN + s + 1

        def item_turns(eng, item, count, body, bases=False):
            at = None
            if bases:
                at = [eng.value_load(meta[0:1, ds(item * 2 + s, 1)], min_val=0, max_val=N - 1) for s in range(2)]
            far = eng.value_load(meta[0:1, ds(item + SIDES, 1)], min_val=0, max_val=N - 1)
            with eng.Fori(0, (far >> 6) + 1) as window:
                turn = eng.snap(count, min_val=0, max_val=ITEMS * WINDOWS - 1)
                body(window, turn, at)
                eng.reg_add(count, count, 1)

        def keep_rows(eng, rows, at, window):
            for s in range(2):
                eng.reg_mov(rows[s], at[s] + window * M)
                eng.reg_alu(rows[s], rows[s], N, ALU.min)

        def all_turns(count):
            return {"val": count, "min_val": 1, "max_val": ITEMS * WINDOWS}

        def counter(eng, name):
            r = eng.alloc_register(name)
            eng.reg_mov(r, 0)
            return r

        block = ctx.enter_context(nc.Block())

        @block.sync
        def _(sp):
            sp.wait_ge(pads_set, 3)
            sp.dma_start(dst_i[:, 0:FULL * T].rearrange("p (b t) -> p b t", t=T), dst_full).then_inc(idx_in, 16)
            sp.dma_start(dst_i[0:TAIL, FULL * T:COLS], dst_tail).then_inc(idx_in, 16)
            sp.dma_start(xs[:, 0:C - 1, :], x[0:(C - 1) * P, :].rearrange("(c p) d -> p c d", p=P)).then_inc(x_in, 16)
            sp.dma_start(xs[0:LAST, C - 1, :], x[(C - 1) * P:N, :]).then_inc(x_in, 16)
            sp.dma_start(coef[:, :], coeffs.rearrange("(a n) -> a n", a=1).broadcast_to([P, NP])).then_inc(small_in, 16)
            sp.dma_start(path_i[:, :], paths.rearrange("(a n) c -> a (n c)", a=1)).then_inc(small_in, 16)

            sp.wait_ge(meta_ready, 1)
            turn_count = counter(sp, "sp_turn")

            def load(item, tail, turn):
                for j in range(2):
                    sp.wait_ge(multiplied, group_before(turn, j * G + G - 1))
                    for s in range(2):
                        rows = TAIL if tail and s else P
                        to = batch(x2_mem, j)[0:rows, s * TB[j] * D:(s + 1) * TB[j] * D]
                        a, b = T0[j] * D, (T0[j] + TB[j]) * D
                        if tail and s:
                            sp.dma_start(to, edge_tail[:, a:b]).then_inc(x2_in[j], 16)
                        else:
                            side = 2 * item + s
                            sp.dma_start(to, edge_full[:, ds(side, 1), a:b].rearrange("p b n -> p (b n)")).then_inc(x2_in[j], 16)

            sp.wait_ge(g_ready, 1)
            with sp.Fori(0, ITEMS - 1) as item:
                item_turns(sp, item, turn_count, lambda window, turn, at: load(item, False, turn))
            item_turns(sp, ITEMS - 1, turn_count, lambda window, turn, at: load(ITEMS - 1, True, turn))

        @block.gpsimd
        def _(pool):
            nc.gpsimd.memset(xs[96:P, C - 1, :], 0.0).then_inc(pads_set, 1)
            pool.wait_ge(pads_set, 1)
            nc.gpsimd.memset(dst_i, NOWHERE).then_inc(pads_set, 1)
            nc.gpsimd.memset(src_i[:, :], 0).then_inc(pads_set, 1)
            nc.gpsimd.iota(iota_i, pattern=[[1, CW]], base=0, channel_multiplier=0).then_inc(iota_done, 1)
            nc.gpsimd.memset(ident, 0.0).then_inc(g_chain, 1)
            pool.wait_ge(g_chain, 1)
            nc.gpsimd.affine_select(out=ident, in_=ident, compare_op=ALU.not_equal, fill=1.0, base=0,
                                    pattern=[[-1, P]], channel_multiplier=1).then_inc(ident_done, 1)
            nc.gpsimd.memset(first_row, 0.0).then_inc(g_chain, 1)
            pool.wait_ge(g_chain, 2)
            nc.gpsimd.memset(first_row[0:1, :], 1.0).then_inc(zeros_set, 1)
            pool.wait_ge(zeros_set, 1)
            nc.gpsimd.memset(acc[:, :], 0.0).then_inc(zeros_set, 1)
            nc.gpsimd.memset(counts, 0.0).then_inc(zeros_set, 1)
            pool.wait_ge(span_ready, 1)
            nc.gpsimd.partition_all_reduce(span_all, span, P, bass.bass_isa.ReduceOp.max).then_inc(span_reduced, 1)
            nc.gpsimd.memset(countsT, 0.0).then_inc(g_chain, 1)
            pool.wait_ge(g_chain, 3)
            pool.wait_ge(ident_done, 1)
            for c in range(C):
                nc.gpsimd.tensor_copy(countsT[:, c, c * P:(c + 1) * P], ident).then_inc(countsT_init, 1)
            pool.wait_ge(zeros_set, 3)
            pool.dma_start(out[N:N + M, :], acc[0:M, :]).then_inc(out_added, 16)

            pool.wait_ge(meta_ready, 1)
            for i in range(2):
                pool.wait_ge(h2_stored[i], 16 * (C // 2))
            pool.wait_ge(xs_stored, 16 * C)
            pool.wait_ge(out_added, 16)
            pool.wait_ge(summed, TURN)
            pool.sem_inc(s_free, 2)
            turn_count = counter(pool, "pool_turn")
            rows = [counter(pool, f"pool_row{s}") for s in range(2)]
            i3_regs = [pool.alloc_register(f"i3_{n}") for n in range(PG)]

            def mix(turn):
                pool.wait_ge(out_added, turn * 32 + 16)
                pool.sem_inc(pool_steps, 1)
                pool.sem_clear(mixed)
                nc.gpsimd.memset(acc[:, :], 0.0).then_inc(mixed, 1)
                step = 1
                for g in range(G):
                    pool.load(i3_regs, i3[0:1, g * PG:(g + 1) * PG])
                    pool.wait_ge(saved, turn * G + g + 1)
                    pool.sem_inc(pool_steps, 1)
                    sums = S[:, g % 2, :].rearrange("p (n u) -> p n u", u=U)
                    c = coef[:, g * PG:(g + 1) * PG].rearrange("p (n a) -> p n a", a=1).broadcast_to([P, PG, U])
                    nc.gpsimd.tensor_tensor(sums, sums, c, ALU.mult).then_inc(mixed, 1)
                    step += 1
                    for n in range(PG):
                        to = pool.snap(i3_regs[n], min_val=0, max_val=D - U)
                        pool.wait_ge(mixed, step)
                        nc.gpsimd.tensor_tensor(acc[:, ds(to, U)], acc[:, ds(to, U)],
                                                S[:, g % 2, n * U:(n + 1) * U], ALU.add).then_inc(mixed, 1)
                        step += 1
                    pool.wait_ge(mixed, step)
                    pool.sem_inc(s_free, 1)
                row = [pool.snap(r, min_val=0, max_val=N) for r in rows]
                pool.dma_start(out[ds(row[0], M), :], acc[0:M, :], accum_op=ALU.add).then_inc(out_added, 16)
                pool.wait_ge(out_added, turn * 32 + 32)
                pool.sem_inc(pool_steps, 1)
                pool.dma_start(out[ds(row[1], M), :], acc[M:P, :], accum_op=ALU.add).then_inc(out_added, 16)

            def gather_turn(item, window, turn, at):
                for j in range(2):
                    pool.wait_ge(multiplied, group_before(turn, j * G + G - 1))
                    now = src_now[:, 2 * T0[j]:2 * (T0[j] + TB[j])]
                    src = src_i[:, :].rearrange("p (b t) -> p b t", t=T)[:, ds(2 * item, 2), T0[j]:T0[j] + TB[j]]
                    nc.gpsimd.tensor_copy(now.rearrange("p (s t) -> p s t", s=2), src).then_inc(idx_copied, 1)
                    pool.wait_ge(idx_copied, turn * 2 + j + 1)
                    pool.sem_inc(pool_steps, 1)
                    for t in range(2 * TB[j]):
                        pool.indirect_dma_start(x1[j][:, t, :], None, h2_dram[:, :],
                                                bass.IndirectOffsetOnAxis(ap=now[:, t:t + 1].bitcast(u32), axis=0)
                                                ).then_inc(x1_in[j], 16)
                mix(turn)
                keep_rows(pool, rows, at, window)

            with pool.Fori(0, ITEMS) as item:
                item_turns(pool, item, turn_count, lambda w, turn, at: gather_turn(item, w, turn, at), bases=True)
            total = pool.snap(**all_turns(turn_count))
            mix(total)
            pool.wait_ge(out_added, total * 32 + 48)

        @block.vector
        def _(dve):
            chain = [0]

            def link(ins):
                chain[0] += 1
                ins.then_inc(v_chain, 1)
                dve.wait_ge(v_chain, chain[0])

            dve.wait_ge(iota_done, 1)
            nc.vector.tensor_copy(iota_h, iota_i).then_inc(consts_ready, 1)
            nc.vector.tensor_scalar(shift_w[:, :], iota_i[:, 0:WINDOWS], float(M), None, ALU.mult).then_inc(consts_ready, 1)
            nc.vector.tensor_copy(iota_f[:, :], iota_i[:, 0:M]).then_inc(consts_ready, 1)

            dve.wait_ge(idx_in, 64)
            nc.vector.tensor_copy(src_f, src_i[:, :])
            link(nc.vector.tensor_copy(dst_f[:, :], dst_i))
            link(nc.vector.tensor_scalar(tmp_c, dst_f[:, :], -1.0, None, ALU.mult))
            nc.vector.tensor_reduce(span[:, 0:SIDES], tmp_c.rearrange("p (i t) -> p i t", t=T), AX.X, ALU.max)
            link(nc.vector.tensor_scalar(dst_i.bitcast(fp32), dst_f[:, :], float(NOWHERE), None, ALU.is_lt))
            link(nc.vector.tensor_tensor(tmp_c, dst_i.bitcast(fp32), dst_f[:, :], ALU.mult))
            nc.vector.tensor_reduce(span[:, SIDES:2 * SIDES], tmp_c.rearrange("p (i t) -> p i t", t=T), AX.X,
                                    ALU.max).then_inc(span_ready, 1)

            dve.wait_ge(x_in, 32)
            for c in range(C):
                last = nc.vector.bn_stats(stats[:, c, :], xs[:, c, :])
            link(last)
            for c in range(C):
                last = nc.vector.bn_aggr(mv[:, c, :], stats[:, c, :])
            link(last)
            nc.vector.tensor_scalar(rstd, mv[:, :, 1], EPS, None, ALU.add).then_inc(var_ready, 1)

            dve.wait_ge(span_reduced, 1)
            link(nc.vector.tensor_scalar(base_f[:, :], span_all[:, 0:SIDES], -1.0, None, ALU.mult))
            link(nc.vector.tensor_tensor(tmp_c[:, 0:SIDES], span_all[:, SIDES:2 * SIDES], base_f[:, :], ALU.subtract))
            link(nc.vector.tensor_reduce(tmp_c[:, SIDES:SIDES + ITEMS],
                                         tmp_c[:, 0:SIDES].rearrange("p (i s) -> p i s", s=2), AX.X, ALU.max))
            nc.vector.tensor_copy(meta[:, 0:SIDES], base_f[:, :])
            nc.vector.tensor_copy(meta[:, SIDES:SIDES + ITEMS], tmp_c[:, SIDES:SIDES + ITEMS]).then_inc(meta_ready, 1)

            dve.wait_ge(root_ready, 1)
            link(nc.vector.reciprocal(rstd, rstd))
            link(nc.vector.tensor_tensor(shift, mv[:, :, 0], rstd, ALU.mult))
            nc.vector.tensor_scalar(shift, shift, -1.0, None, ALU.mult).then_inc(norm_ready, 1)

            for k in range(K):
                dve.wait_ge(w_transposed, k + 1)
                nc.vector.tensor_copy(wT[:, k, :], ps[3 + k % 2]).then_inc(wT_ready, 1)

            dve.wait_ge(consts_ready, 3)
            dve.wait_ge(countsT_init, C)
            turn_count = counter(dve, "dve_turn0")
            rows = [counter(dve, f"dve_row{s}") for s in range(2)]

            def add_counts(turn):
                dve.wait_ge(counts_transposed, turn + 2)
                for s in range(2):
                    row = dve.snap(rows[s], min_val=0, max_val=N)
                    dve.wait_ge(counts_added, turn * 2 + (2 + s))
                    to = countsT[:, :, ds(row, M)]
                    nc.vector.tensor_tensor(to, psT[:, :, s * M:(s + 1) * M], to, ALU.add).then_inc(counts_added, 1)

            def source_turn(item, window, turn, at):
                for n in range(TI):
                    dve.wait_ge(hots_used, turn * TI + (n + 1))
                    col = (item * 2 + n % 2) * T + n // 2
                    nc.vector.tensor_scalar(src_hot[:, n % RING, :], iota_h, src_f[:, ds(col, 1)], None,
                                            ALU.is_equal).then_inc(hots_ready, 1)
                    if n == RING:
                        add_counts(turn)
                keep_rows(dve, rows, at, window)

            with dve.Fori(0, ITEMS) as item:
                item_turns(dve, item, turn_count, lambda w, turn, at: source_turn(item, w, turn, at), bases=True)
            total = dve.snap(**all_turns(turn_count))
            add_counts(total)

            dve.wait_ge(counts_added, total * 2 + 4)
            nc.vector.tensor_reduce(deg, countsT, AX.X, ALU.add).then_inc(g_ready, 1)
            dve.wait_ge(g_ready, 1)
            nc.vector.tensor_scalar(dis, deg, 1.0, None, ALU.mult).then_inc(var_ready, 1)
            dve.wait_ge(root_ready, 2)
            nc.vector.reciprocal(dis, dis).then_inc(g_ready, 1)
            dve.wait_ge(g_ready, 2)
            dve.wait_ge(hw_saved, C + 1)
            for c in range(C):
                nc.vector.tensor_scalar(hw[:, c + 1, :], hw[:, c + 1, :], dis[:, c:c + 1], None, ALU.mult).then_inc(g_ready, 1)

            for c in range(C):
                dve.wait_ge(y_ready, c + 1)
                nc.vector.tensor_tensor(xs[:, c, :], xs[:, c, :], y[:, c % 2, :], ALU.add).then_inc(xs_ready, 1)
                dve.wait_ge(xs_ready, 5 * c + 1)
                nc.vector.bn_stats(stats2, xs[:, c, :]).then_inc(xs_ready, 1)
                dve.wait_ge(xs_ready, 5 * c + 2)
                nc.vector.bn_aggr(mv2, stats2).then_inc(xs_ready, 1)
                dve.wait_ge(xs_ready, 5 * c + 3)
                if c >= 2:
                    dve.wait_ge(h2_ready, c - 1)
                nc.vector.tensor_scalar(rs2[:, c % 2, 0:1], mv2[:, 1:2], EPS, None, ALU.add).then_inc(var_ready, 1)
                dve.wait_ge(root_ready, c + 3)
                nc.vector.reciprocal(rs2[:, c % 2, 0:1], rs2[:, c % 2, 0:1]).then_inc(xs_ready, 1)
                dve.wait_ge(xs_ready, 5 * c + 4)
                nc.vector.tensor_scalar(rs2[:, c % 2, 1:2], mv2[:, 0:1], rs2[:, c % 2, 0:1], -1.0, ALU.mult,
                                        ALU.mult).then_inc(xs_ready, 1)

            dve.wait_ge(small_in, 48)
            pv = path_i[:, :].rearrange("a (n c) -> a n c", c=3)
            nc.vector.tensor_scalar(i12[:, :, :], pv[:, :, 0:2], U, None, ALU.mult)
            link(nc.vector.tensor_scalar(i3[:, :], pv[:, :, 2], U, None, ALU.mult))

            dve.sem_inc(multiplied, TURN)
            turn_count = counter(dve, "dve_turn1")
            regs = [dve.alloc_register(f"i12_{n}") for n in range(PG)]

            def product_turn(window, turn, at):
                for j in range(2):
                    for g in range(G):
                        s = j * G + g
                        for half in range(2):
                            p0 = g * PG + half * (PG // 2)
                            dve.load(regs, i12[0:1, p0:p0 + PG // 2, :].rearrange("a n c -> a (n c)"))
                            if g == 0 and half == 0:
                                dve.wait_ge(x1_in[j], turn * (32 * TB[j]) + 32 * TB[j])
                                dve.wait_ge(x2_in[j], turn * 32 + 32)
                            if half == 0:
                                dve.wait_ge(summed, group(turn, s - 2))
                            for n in range(PG // 2):
                                a = dve.snap(regs[2 * n], min_val=0, max_val=D - U)
                                b = dve.snap(regs[2 * n + 1], min_val=0, max_val=D - U)
                                last = nc.vector.tensor_tensor(
                                    q[s % 2][:, 0:2 * TB[j], half * (PG // 2) + n, :],
                                    x1[j][:, :, ds(a, U)], x2[j][:, :, ds(b, U)], ALU.mult)
                        last.then_inc(multiplied, 1)

            with dve.Fori(0, ITEMS) as item:
                item_turns(dve, item, turn_count, product_turn)

        @block.scalar
        def _(act):
            act.wait_ge(pads_set, 3)
            act.dma_start(src_i[:, 0:FULL * T].rearrange("p (b t) -> p b t", t=T), src_full).then_inc(idx_in, 16)
            act.dma_start(src_i[0:TAIL, FULL * T:COLS], src_tail).then_inc(idx_in, 16)
            act.dma_start(w_rows, W.rearrange("(k p) d -> p k d", p=P)).then_inc(w_in, 16)
            act.dma_start(bias_b, bias.rearrange("(a n) -> a n", a=1).broadcast_to([P, D])).then_inc(small_in, 16)

            act.wait_ge(var_ready, 1)
            nc.scalar.activation(rstd, rstd, ACT.Sqrt).then_inc(root_ready, 1)
            act.wait_ge(norm_ready, 1)
            act.wait_ge(meta_ready, 1)
            act.wait_ge(consts_ready, 3)
            act.wait_ge(zeros_set, 3)
            turn_count = counter(act, "act_turn0")

            def distances(item, window, turn, chain):
                act.wait_ge(chain, turn * 4 + 4)
                for s in range(2):
                    last = nc.scalar.activation(rel[:, 0, s * T:(s + 1) * T], dst_f[:, ds((item * 2 + s) * T, T)],
                                                ACT.Identity, scale=-1.0, bias=base_f[:, ds(item * 2 + s, 1)])
                last.then_inc(chain, 1)
                act.wait_ge(chain, turn * 4 + 5)
                nc.scalar.activation(rel[:, 1, :], rel[:, 0, :], ACT.Identity,
                                     bias=shift_w[:, ds(window, 1)]).then_inc(chain, 1)
                act.wait_ge(chain, turn * 4 + 6)

            def destinations(j, hots, turn, chain, ready):
                for s in range(2):
                    for t in range(TB[j]):
                        at = s * T + T0[j] + t
                        last = nc.scalar.activation(hots[:, s * TB[j] + t, :], iota_f[:, :], ACT.Abs, bias=rel[:, 1, at:at + 1])
                last.then_inc(chain, 1)
                act.wait_ge(chain, turn * 4 + (7 + j))
                nc.scalar.activation(hots, hots, ACT.Relu, scale=-1.0, bias=1.0).then_inc(ready, 1)

            def save_features(c):
                act.wait_ge(hw_summed, c + 1)
                to = hw[:, c, :] if isinstance(c, int) else hw[:, ds(c, 1), :].rearrange("p c d -> p (c d)")
                nc.scalar.activation(to, ps[7], ACT.Copy).then_inc(hw_saved, 1)

            def normalise(c):
                act.wait_ge(h1_transposed, c + 1)
                nc.scalar.activation(h1, xs[:, ds(c, 1), :].rearrange("p c d -> p (c d)"), ACT.Relu,
                                     bias=shift[:, ds(c, 1)], scale=rstd[:, ds(c, 1)]).then_inc(h1_ready, 1)

            def save_transposed(c):
                act.wait_ge(h1_transposed, c + 2)
                act.wait_ge(hw_summed, c + 1)
                nc.scalar.activation(h1T, ps[6], ACT.Copy).then_inc(h1T_ready, 1)

            def save_counts(turn):
                act.wait_ge(counts_transposed, turn + 1)
                act.wait_ge(hots_used, turn * TI + RING)
                for b in range(3):
                    n = min(BANK, N - BANK * b)
                    nc.scalar.activation(counts[:, BANK * b:BANK * b + n], ps[b][:, 0:n], ACT.Copy).then_inc(counts_saved, 1)

            def count_turn(item, window, turn, at):
                distances(item, window, turn, a_chain0)
                for j in range(2):
                    act.wait_ge(hots_used, turn * TI + (RING - TI + 2 * (T0[j] + TB[j])))
                    destinations(j, dst_hot[j], turn, a_chain0, dst_ready)
                    if j == 0:
                        save_counts(turn)

            act.sem_inc(a_chain0, 4)
            with act.Fori(0, C) as item:
                normalise(item)
                item_turns(act, item, turn_count, lambda w, turn, at: count_turn(item, w, turn, at))
                save_features(item)
                save_transposed(item)
            with act.Fori(C, ITEMS) as item:
                item_turns(act, item, turn_count, lambda w, turn, at: count_turn(item, w, turn, at))
            save_features(C)
            save_counts(act.snap(**all_turns(turn_count)))

            act.wait_ge(var_ready, 2)
            nc.scalar.activation(dis, dis, ACT.Sqrt).then_inc(root_ready, 1)
            act.wait_ge(g_ready, 2 + C)
            for c in range(C):
                rows = P if c < C - 1 else LAST
                act.wait_ge(agg_summed, c + 1)
                nc.scalar.activation(y[:, c % 2, :], ps[6 + c % 2], ACT.Relu, scale=dis[:, c:c + 1]).then_inc(y_ready, 1)
                act.wait_ge(var_ready, c + 3)
                nc.scalar.activation(rs2[:, c % 2, 0:1], rs2[:, c % 2, 0:1], ACT.Sqrt).then_inc(root_ready, 1)
                act.wait_ge(xs_ready, 5 * c + 5)
                if c >= 2:
                    act.wait_ge(h2_stored[c % 2], 16 * (c // 2))
                nc.scalar.activation(h2[:, c % 2, :], xs[:, c, :], ACT.Relu, bias=rs2[:, c % 2, 1:2],
                                     scale=rs2[:, c % 2, 0:1]).then_inc(h2_ready, 1)
                act.dma_start(out[c * P:c * P + rows, :], xs[0:rows, c, :]).then_inc(xs_stored, 16)
                act.wait_ge(h2_ready, c + 1)
                act.dma_start(h2_dram[c * P:c * P + rows, :], h2[0:rows, c % 2, :]).then_inc(h2_stored[c % 2], 16)

            act.sem_inc(a_chain1, 4)
            turn_count = counter(act, "act_turn1")

            def save(turn):
                for g in range(G):
                    act.wait_ge(summed, group_before(turn, G + g))
                    act.wait_ge(s_free, turn * G + g + 1)
                    nc.scalar.activation(S[:, g % 2, :], ps[g], ACT.Copy).then_inc(saved, 1)

            def sum_turn(item, window, turn, at):
                distances(item, window, turn, a_chain1)
                for j in range(2):
                    act.wait_ge(summed, group_before(turn, j * G + G - 1))
                    destinations(j, hot[j].rearrange("p s t n -> p (s t) n"), turn, a_chain1, hot_ready)
                    if j == 0:
                        save(turn)

            with act.Fori(0, ITEMS) as item:
                item_turns(act, item, turn_count, lambda w, turn, at: sum_turn(item, w, turn, at))
            save(act.snap(**all_turns(turn_count)))

        @block.tensor
        def _(pe):
            pe.wait_ge(ident_done, 1)
            pe.wait_ge(w_in, 16)
            for k in range(K):
                if k >= 2:
                    pe.wait_ge(wT_ready, k - 1)
                for o in range(K):
                    last = nc.tensor.transpose(ps[3 + k % 2][:, o * P:(o + 1) * P], w_rows[:, o, k * P:(k + 1) * P], ident)
                last.then_inc(w_transposed, 1)

            pe.wait_ge(meta_ready, 1)
            pe.wait_ge(wT_ready, K)
            pe.wait_ge(zeros_set, 3)
            pe.wait_ge(small_in, 48)
            pe.sem_inc(counts_added, 2)
            pe.sem_inc(h1_transposed, 1)
            pe.sem_inc(h1T_ready, 1)
            pe.sem_inc(counts_transposed, 1)
            nc.tensor.matmul(ps[7], acc[:, 0:P], acc[:, :], start=True, stop=True).then_inc(hw_summed, 1)
            for b in range(3):
                last = nc.tensor.matmul(ps[b], acc[:, 0:P], acc[:, :], start=True, stop=True)
            last.then_inc(hots_used, RING)
            turn_count = counter(pe, "pe_turn0")

            def transpose_features(c):
                pe.wait_ge(h1_ready, c + 1)
                pe.wait_ge(h1T_ready, c + 1)
                for k in range(K):
                    last = nc.tensor.transpose(ps[6][:, k * P:(k + 1) * P], h1[:, k * P:(k + 1) * P], ident)
                last.then_inc(h1_transposed, 1)

            def multiply_features(c):
                pe.wait_ge(hw_saved, c + 1)
                nc.tensor.matmul(ps[7], first_row, bias_b, start=True, stop=False)
                pe.wait_ge(h1T_ready, c + 2)
                for k in range(K):
                    last = nc.tensor.matmul(ps[7], h1T[:, k * P:(k + 1) * P], wT[:, k, :], start=False, stop=(k == K - 1))
                last.then_inc(hw_summed, 1)

            def transpose_counts(turn):
                pe.wait_ge(counts_added, turn * 2 + 2)
                for c in range(C):
                    last = nc.tensor.transpose(psT[:, c, :], counts[:, c * P:(c + 1) * P], ident)
                last.then_inc(counts_transposed, 1)

            def count_turn(window, turn, at):
                for n in range(TI):
                    t, s = n // 2, n % 2
                    j = 0 if t < TB[0] else 1
                    if n == 2 * T0[j]:
                        pe.wait_ge(dst_ready, turn * 2 + (j + 1))
                    pe.wait_ge(hots_ready, turn * TI + (n + 1))
                    for b in range(3):
                        w = min(BANK, N - BANK * b)
                        if n == 0:
                            pe.wait_ge(counts_saved, turn * 3 + (b + 1))
                        last = nc.tensor.matmul(ps[b][s * M:(s + 1) * M, 0:w], dst_hot[j][:, s * TB[j] + t - T0[j], :],
                                                src_hot[:, n % RING, BANK * b:BANK * b + w],
                                                start=(t == 0), stop=(t == T - 1))
                    last.then_inc(hots_used, 1)
                    if n == 5:
                        transpose_counts(turn)

            with pe.Fori(0, C) as item:
                transpose_features(item)
                item_turns(pe, item, turn_count, count_turn)
                multiply_features(item)
            with pe.Fori(C, ITEMS) as item:
                item_turns(pe, item, turn_count, count_turn)
            total = pe.snap(**all_turns(turn_count))
            pe.wait_ge(counts_saved, total * 3 + 3)
            transpose_counts(total)

            for c in range(C):
                if c >= 2:
                    pe.wait_ge(y_ready, c - 1)
                for m in range(C):
                    if c == 0:
                        pe.wait_ge(g_ready, 3 + m)
                    last = nc.tensor.matmul(ps[6 + c % 2], countsT[:, m, c * P:(c + 1) * P], hw[:, m + 1, :],
                                            start=(m == 0), stop=(m == C - 1))
                last.then_inc(agg_summed, 1)

            turn_count = counter(pe, "pe_turn1")
            for g in range(G):
                last = nc.tensor.matmul(ps[g], acc[:, 0:P], acc[:, :], start=True, stop=True)
            last.then_inc(summed, TURN)

            def sum_turn(window, turn, at):
                for j in range(2):
                    pe.wait_ge(hot_ready, turn * 2 + (j + 1))
                    for g in range(G):
                        slot = j * G + g
                        pe.wait_ge(multiplied, group(turn, slot))
                        if j == 0:
                            pe.wait_ge(saved, turn * G + g + 1)
                        for t in range(TB[j]):
                            for s in range(2):
                                last = nc.tensor.matmul(ps[g][s * M:(s + 1) * M, :], hot[j][:, s, t, :],
                                                        q[slot % 2][:, s * TB[j] + t, :, :].rearrange("p n u -> p (n u)"),
                                                        start=(j == 0 and t == 0), stop=(j == 1 and t == TB[j] - 1))
                        last.then_inc(summed, 1)

            with pe.Fori(0, ITEMS) as item:
                item_turns(pe, item, turn_count, sum_turn)


_INS = ["x", "src", "dst", "edge_attr_512", "L0_gnn_W", "L0_gnn_b", "L1_gnn_path_coeffs", "L1_gnn_path_indices"]


def kernel(**inputs):
    import numpy as _np
    import concourse.bacc as _bacc
    from concourse import mybir as _mybir
    from concourse.bass_utils import run_bass_kernel_spmd as _run

    nc = _bacc.Bacc("TRN2", target_bir_lowering=False, num_devices=1)
    arrays, args = {}, []
    for name in _INS:
        a = _np.ascontiguousarray(inputs[name])
        arrays[f"in_{name}"] = a
        args.append(nc.dram_tensor(f"in_{name}", a.shape, _mybir.dt.from_np(a.dtype), kind="ExternalInput").ap())
    n, d = arrays["in_x"].shape
    args.append(nc.dram_tensor("out_0", (n + 64, d), _mybir.dt.float32, kind="ExternalOutput").ap())
    gnn_layers_kernel(nc, *args)
    r = _run(nc, [arrays], core_ids=[0])
    return r.results[0]["out_0"][:n]
```

```python
import concourse.bass as bass
from concourse import mybir
from contextlib import ExitStack


def gnn_layers_kernel(nc, x, src, dst, edge_attr, W, bias, coeffs, paths, out):
    fp32, bf16, fp16 = mybir.dt.float32, mybir.dt.bfloat16, mybir.dt.float16
    i32, i16, u32 = mybir.dt.int32, mybir.dt.int16, mybir.dt.uint32
    ALU, ACT, AX = mybir.AluOpType, mybir.ActivationFunctionType, mybir.AxisListType
    ds = bass.ds

    P = 128
    N, D = x.shape
    E = edge_attr.shape[0]
    NP = coeffs.shape[0]
    U = 32
    EPS = 1e-5
    C = -(-N // P)
    assert C % 2 == 0
    LAST = N - (C - 1) * P
    K = D // P
    T = 15
    TB = [8, 7]
    T0 = [0, 8]
    TI = 2 * T
    M = P // 2
    ITEMS = -(-E // (P * TI))
    FULL = E // (P * T)
    TAIL = (E - FULL * P * T) // T
    assert FULL == 2 * ITEMS - 1 and FULL * P * T + TAIL * T == E
    SIDES = 2 * ITEMS
    COLS = ITEMS * TI
    WINDOWS = N // M + 2
    G = 4
    PG = NP // G
    SURE = PG - PG // G
    PAIR = 2
    assert PG - SURE == 2 * PAIR
    TURN = 2 * G
    QT = 2 * TB[0]
    RING = 15
    DEG_V = 4
    ROWS_A = 12
    LATER = 7
    CW = C * P
    AW = CW + M
    KW = C * M
    AWAY = 4096
    EXACT = 256
    PARTS = 3
    AHEAD = 4
    NOWHERE = 8192
    BANK = 512

    src_full = src[0:FULL * P * T].rearrange("(b p t) -> p b t", p=P, t=T)
    dst_full = dst[0:FULL * P * T].rearrange("(b p t) -> p b t", p=P, t=T)
    src_tail = src[FULL * P * T:E].rearrange("(p t) -> p t", t=T)
    dst_tail = dst[FULL * P * T:E].rearrange("(p t) -> p t", t=T)
    edge_full = edge_attr[0:FULL * P * T, :].rearrange("(b p t) d -> p b (t d)", p=P, t=T)
    edge_tail = edge_attr[FULL * P * T:E, :].rearrange("(p t) d -> p (t d)", t=T)
    h2_dram = nc.dram_tensor("h2_rows", (N, D), fp32).ap()

    ctx = ExitStack()
    with ctx:
        def sb(name, shape, dt):
            return ctx.enter_context(nc.sbuf_tensor(name, shape, dt))

        def sem(name):
            return ctx.enter_context(nc.semaphore(name))

        x1_mem = sb("x1_mem", [P, TI * D], fp32)
        x2_mem = sb("x2_mem", [P, TI * D], fp32)
        q_mem = sb("q_mem", [P, 2 * QT * PG * U], fp32)
        hot_mem = sb("hot_mem", [P, TI * M], fp32)

        def batch(mem, j):
            at, n = 2 * T0[j] * D, 2 * TB[j] * D
            return mem[:, at:at + n]

        x1 = [batch(x1_mem, j).rearrange("p (t d) -> p t d", d=D) for j in range(2)]
        x2 = [batch(x2_mem, j).rearrange("p (t d) -> p t d", d=D) for j in range(2)]
        q = [q_mem[:, s * QT * PG * U:(s + 1) * QT * PG * U].rearrange("p (t n u) -> p t n u", n=PG, u=U)
             for s in range(2)]
        hot = [hot_mem[:, 2 * T0[j] * M:2 * (T0[j] + TB[j]) * M].rearrange("p (s t n) -> p s t n", s=2, n=M)
               for j in range(2)]

        class Carve:
            def __init__(self, mem):
                self.mem, self.at = mem, 0

            def take(self, words):
                self.at += words
                return self.mem[:, self.at - words:self.at]

        in_x2, in_x1, in_q = Carve(x2_mem), Carve(x1_mem), Carve(q_mem)
        w_rows = in_x2.take(K * D).rearrange("p (k n) -> p k n", k=K)
        wT = in_x2.take(K * D).rearrange("p (k n) -> p k n", k=K)
        h1 = in_x2.take(D)
        h1T = in_x2.take(D)
        key_hot = in_x2.take(RING * KW // 2).bitcast(bf16).rearrange("p (r n) -> p r n", r=RING)
        iota_h = in_x2.take(KW // 2).bitcast(fp16)
        row_hot = [hot_mem[:, s * T * P // 2:(s + 1) * T * P // 2].bitcast(bf16).rearrange("p (t n) -> p t n", n=P)
                   for s in range(2)]

        in_agg = Carve(x2_mem)
        counts_b = in_agg.take(C * CW // 2).bitcast(bf16).rearrange("p (c n) -> p c n", c=C)
        parts = [in_agg.take(C * D // 2).bitcast(bf16).rearrange("p (c n) -> p c n", c=C) for i in range(PARTS)]

        hw = in_x1.take((C + 1) * D).rearrange("p (c n) -> p c n", c=C + 1)
        xs = in_x1.take(C * D).rearrange("p (c n) -> p c n", c=C)
        keys_mem = in_x1.take(CW)
        src_f = in_x1.take(COLS)
        src_i = in_x1.take(COLS).bitcast(i32)
        path_rows_i = in_x1.take(NP * 3).bitcast(i32)
        path_cols_i = in_x1.take(3).bitcast(i32)
        path_vals = in_x1.take(5)
        places = in_x1.take(2)
        stats = in_x1.take(C * 6).rearrange("p (c n) -> p c n", c=C)
        mv = in_x1.take(C * 2).rearrange("p (c n) -> p c n", c=C)
        rstd = in_x1.take(C)
        shift = in_x1.take(C)
        deg = in_x1.take(C)
        dis = in_x1.take(C)
        y = in_x1.take(2 * D).rearrange("p (s n) -> p s n", s=2)
        h2 = in_x1.take(2 * D).rearrange("p (s n) -> p s n", s=2)
        rests = [y[:, 0, :], y[:, 1, :], h2[:, 0, :], h2[:, 1, :]]
        deg_max = in_x1.take(1)
        deg_max_all = in_x1.take(1)
        deg_max_i = in_x1.take(1).bitcast(i32)
        stats2 = in_x1.take(6)
        mv2 = in_x1.take(2)
        rs2 = in_x1.take(2 * 2).rearrange("p (s n) -> p s n", s=2)

        in_keys = Carve(keys_mem)
        src_chunk = in_keys.take(COLS)
        minus_row = in_keys.take(COLS)
        src_row = in_keys.take(COLS)
        keys = in_keys.take(TI)
        in_window = in_keys.take(TI)
        clamped = in_keys.take(TI)
        keys_next = in_keys.take(TI)

        in_counts = Carve(keys_mem)
        path_rows = in_counts.take(NP * 3).rearrange("p (n c) -> p n c", c=3)
        path_cols = in_counts.take(3)
        number = in_counts.take(NP)
        partition = in_counts.take(1)
        key_row = in_counts.take(NP)
        key_col = in_counts.take(1)
        same = in_counts.take(NP)
        before = in_counts.take(NP)
        repeats = in_counts.take(NP)
        first = in_counts.take(NP)
        merged = in_counts.take(NP)
        running = [in_counts.take(2 * NP) for i in range(2)]
        kept = in_counts.take(1)
        place_rows = in_x1.take(2 * NP).rearrange("p (k n) -> p k n", k=2)
        spread = in_x1.take(NP)
        in_src = Carve(src_f)
        laid = in_src.take(5 * NP).rearrange("p (k n) -> p k n", k=5)
        laid_sum = in_counts.take(5 * NP).rearrange("p (k n) -> p k n", k=5)

        countsT = in_q.take(C * AW).rearrange("p (c n) -> p c n", c=C)
        iota_i = in_q.take(CW).bitcast(i32)
        ident = in_q.take(P)
        dst_i = in_q.take(COLS).bitcast(i32)
        tmp_c = in_q.take(COLS)
        span = in_q.take(2 * SIDES)
        span_all = in_q.take(2 * SIDES)
        first_row = in_q.take(P)
        bias_b = in_q.take(D)

        dst_f = sb("dst_f", [P, COLS], fp32)
        src_16 = sb("src_16", [P, COLS], i16)
        src_now = sb("src_now", [P, TI], i32)
        iota_f = sb("iota_f", [P, M], fp32)
        shift_w = sb("shift_w", [P, WINDOWS], fp32)
        base_f = sb("base_f", [P, SIDES], fp32)
        meta = sb("meta", [P, SIDES + ITEMS + 1], i32)
        n_kept = meta[0:1, SIDES + ITEMS:SIDES + ITEMS + 1]
        coef = sb("coef", [P, NP], fp32)
        i12 = sb("i12", [1, NP, 2], i16)
        i3 = sb("i3", [1, NP], i16)
        slot_at = sb("slot_at", [1, PG], i16)
        rel = sb("rel", [P, 2, TI], fp32)
        S = sb("S", [P, NP * U], fp32)
        acc = sb("acc", [P, D], fp32)
        acc_odd = sb("acc_odd", [P, D], fp32)[:, :]

        psum = ctx.enter_context(nc.psum_tensor("psum", [P, 8 * BANK], fp32))
        ps = [psum[:, i * BANK:(i + 1) * BANK] for i in range(8)]
        key_sums = [psum[:, 2 * s * BANK:2 * s * BANK + KW] for s in range(2)]

        x_in, idx_in, w_in, small_in = sem("x_in"), sem("idx_in"), sem("w_in"), sem("small_in")
        pads_set, iota_done, ident_done = sem("pads_set"), sem("iota_done"), sem("ident_done")
        consts_ready, zeros_set, countsT_init = sem("consts_ready"), sem("zeros_set"), sem("countsT_init")
        span_ready, span_reduced, meta_ready = sem("span_ready"), sem("span_reduced"), sem("meta_ready")
        v_chain, a_chain0, a_chain1, g_chain = sem("v_chain"), sem("a_chain0"), sem("a_chain1"), sem("g_chain")
        var_ready, root_ready = sem("var_ready"), sem("root_ready")
        norm_ready, h1_ready, h1_transposed = sem("norm_ready"), sem("h1_ready"), sem("h1_transposed")
        h1T_ready, w_transposed, wT_ready = sem("h1T_ready"), sem("w_transposed"), sem("wT_ready")
        hw_summed, hw_saved, rows_ready = sem("hw_summed"), sem("hw_saved"), sem("rows_ready")
        hots_ready, hots_used = sem("hots_ready"), sem("hots_used")
        counts_b_ready, deg_max_ready, deg_max_known = sem("counts_b_ready"), sem("deg_max_ready"), sem("deg_max_known")
        parts_in = [sem(f"part{i}_ready") for i in range(PARTS)]
        rest_ready = sem("rest_ready")
        degrees_ready, countsT_cleared = sem("degrees_ready"), sem("countsT_cleared")
        counts_added, keys_ready, key_step = sem("counts_added"), sem("keys_ready"), sem("key_step")
        g_ready, agg_summed, y_ready = sem("g_ready"), sem("agg_summed"), sem("y_ready")
        xs_ready, h2_ready = sem("xs_ready"), sem("h2_ready")
        h2_stored = [sem(f"h2_stored{i}") for i in range(2)]
        xs_stored = sem("xs_stored")
        x1_in = [sem(f"x1_in{j}") for j in range(2)]
        x2_in = [sem(f"x2_in{j}") for j in range(2)]
        multiplied, summed = sem("multiplied"), sem("summed")
        hot_ready, saved, s_free = sem("hot_ready"), sem("saved"), sem("s_free")
        idx_copied, out_added = sem("idx_copied"), sem("out_added")
        paths_in, place_rows_ready, places_ready = sem("paths_in"), sem("place_rows_ready"), sem("places_ready")
        paths_ready, path_step, steps_reg = sem("paths_ready"), sem("path_step"), sem("steps_reg")
        mixed, q_zeroed = sem("mixed"), sem("q_zeroed")
        pool_steps = sem("pool_steps")

        def agg_bank(c):
            return c if c < AHEAD else 4 + c % 4

        def position(rank):
            if rank < G * SURE:
                return rank // SURE * PG + rank % SURE
            r = rank - G * SURE
            pair_of, g, n = r // (G * PAIR), r // PAIR % G, r % PAIR
            return g * PG + SURE + pair_of * PAIR + n

        def group(turn, s):
            return turn * TURN + TURN + s + 1

        def group_before(turn, s):
            return turn * TURN + s + 1

        def item_turns(eng, item, count, body, bases=False):
            at = None
            if bases:
                at = [eng.value_load(meta[0:1, ds(item * 2 + s, 1)], min_val=0, max_val=N - 1) for s in range(2)]
            far = eng.value_load(meta[0:1, ds(item + SIDES, 1)], min_val=0, max_val=N - 1)
            with eng.Fori(0, (far >> 6) + 1) as window:
                turn = eng.snap(count, min_val=0, max_val=ITEMS * WINDOWS - 1)
                body(window, turn, at)
                eng.reg_add(count, count, 1)

        def keep_rows(eng, rows, at, window):
            for s in range(2):
                eng.reg_mov(rows[s], at[s] + window * M)
                eng.reg_alu(rows[s], rows[s], N, ALU.min)

        def all_turns(count):
            return {"val": count, "min_val": 1, "max_val": ITEMS * WINDOWS}

        def counter(eng, name):
            r = eng.alloc_register(name)
            eng.reg_mov(r, 0)
            return r

        block = ctx.enter_context(nc.Block())

        @block.sync
        def _(sp):
            sp.wait_ge(pads_set, 5)
            sp.dma_start(dst_i[:, 0:FULL * T].rearrange("p (b t) -> p b t", t=T), dst_full).then_inc(idx_in, 16)
            sp.dma_start(dst_i[0:TAIL, FULL * T:COLS], dst_tail).then_inc(idx_in, 16)
            sp.dma_start(xs[:, 0:C - 1, :], x[0:(C - 1) * P, :].rearrange("(c p) d -> p c d", p=P)).then_inc(x_in, 16)
            sp.dma_start(xs[0:LAST, C - 1, :], x[(C - 1) * P:N, :]).then_inc(x_in, 16)
            sp.dma_start(w_rows, W.rearrange("(k p) d -> p k d", p=P)).then_inc(w_in, 16)
            sp.dma_start(path_vals[0:NP, 4:5], coeffs.rearrange("(n a) -> n a", a=1)).then_inc(paths_in, 16)
            sp.dma_start(path_cols_i[0:NP, :], paths).then_inc(paths_in, 16)
            sp.dma_start(path_rows_i, paths.rearrange("(a n) c -> a (n c)", a=1).broadcast_to([P, NP * 3])).then_inc(paths_in, 16)

            sp.wait_ge(meta_ready, 1)
            turn_count = counter(sp, "sp_turn")

            def load(item, tail, turn):
                for j in range(2):
                    sp.wait_ge(multiplied, group_before(turn, j * G + G - 1))
                    if j:
                        sp.wait_ge(x1_in[0], turn * (32 * TB[0]) + 32 * TB[0])
                    for s in range(2):
                        rows = TAIL if tail and s else P
                        to = batch(x2_mem, j)[0:rows, s * TB[j] * D:(s + 1) * TB[j] * D]
                        a, b = T0[j] * D, (T0[j] + TB[j]) * D
                        if tail and s:
                            sp.dma_start(to, edge_tail[:, a:b]).then_inc(x2_in[j], 16)
                        else:
                            side = 2 * item + s
                            sp.dma_start(to, edge_full[:, ds(side, 1), a:b].rearrange("p b n -> p (b n)")).then_inc(x2_in[j], 16)

            sp.wait_ge(agg_summed, C)
            for i in range(2):
                sp.wait_ge(h2_stored[i], 16 * (C // 2))
            with sp.Fori(0, ITEMS - 1) as item:
                item_turns(sp, item, turn_count, lambda window, turn, at: load(item, False, turn))
            item_turns(sp, ITEMS - 1, turn_count, lambda window, turn, at: load(ITEMS - 1, True, turn))

        @block.gpsimd
        def _(pool):
            nc.gpsimd.memset(xs[96:P, C - 1, :], 0.0).then_inc(pads_set, 1)
            pool.wait_ge(pads_set, 1)
            nc.gpsimd.memset(dst_i, NOWHERE).then_inc(pads_set, 1)
            nc.gpsimd.memset(src_i, 0).then_inc(pads_set, 1)
            nc.gpsimd.memset(path_vals, 0.0).then_inc(pads_set, 1)
            nc.gpsimd.memset(path_cols_i, 0).then_inc(pads_set, 1)
            nc.gpsimd.iota(iota_i, pattern=[[1, CW]], base=0, channel_multiplier=0).then_inc(iota_done, 1)
            nc.gpsimd.memset(ident, 0.0).then_inc(g_chain, 1)
            pool.wait_ge(g_chain, 1)
            nc.gpsimd.affine_select(out=ident, in_=ident, compare_op=ALU.not_equal, fill=1.0, base=0,
                                    pattern=[[-1, P]], channel_multiplier=1).then_inc(ident_done, 1)
            nc.gpsimd.memset(first_row, 0.0).then_inc(g_chain, 1)
            pool.wait_ge(g_chain, 2)
            nc.gpsimd.memset(first_row[0:1, :], 1.0).then_inc(zeros_set, 1)
            pool.wait_ge(zeros_set, 1)
            nc.gpsimd.memset(acc[:, :], 0.0).then_inc(zeros_set, 1)
            nc.gpsimd.memset(countsT[:, 0:C // 2, :], 0.0).then_inc(countsT_cleared, 1)
            pool.wait_ge(span_ready, 1)
            nc.gpsimd.partition_all_reduce(span_all, span, P, bass.bass_isa.ReduceOp.max).then_inc(span_reduced, 1)
            pool.wait_ge(zeros_set, 2)
            pool.dma_start(out[N:N + M, :], acc[0:M, :]).then_inc(out_added, 16)

            pool.wait_ge(meta_ready, 1)
            pool.wait_ge(consts_ready, 4)
            turn_count = counter(pool, "pool_turn0")

            def key_turn(item, window, turn, at):
                def halves(ap):
                    return ap.rearrange("p (s t) -> p s t", t=T)

                pool.sem_clear(key_step)
                nc.gpsimd.tensor_tensor(halves(in_window), halves(dst_f[:, ds(item * TI, TI)]),
                                        base_f[:, ds(item * 2, 2)].rearrange("p (s a) -> p s a", a=1).broadcast_to([P, 2, T]),
                                        ALU.subtract).then_inc(key_step, 1)
                pool.wait_ge(key_step, 1)
                nc.gpsimd.tensor_tensor(in_window, in_window, shift_w[:, ds(window, 1)].broadcast_to([P, TI]),
                                        ALU.subtract).then_inc(key_step, 1)
                pool.wait_ge(key_step, 2)
                nc.gpsimd.tensor_scalar(clamped, in_window, 0.0, float(M - 1), ALU.max, ALU.min).then_inc(key_step, 1)
                nc.gpsimd.tensor_tensor(keys_next, in_window, src_chunk[:, ds(item * TI, TI)], ALU.add).then_inc(key_step, 1)
                pool.wait_ge(key_step, 4)
                nc.gpsimd.tensor_tensor(clamped, clamped, in_window, ALU.subtract).then_inc(key_step, 1)
                pool.wait_ge(key_step, 5)
                nc.gpsimd.tensor_scalar(clamped, clamped, float(AWAY), None, ALU.mult).then_inc(key_step, 1)
                pool.wait_ge(key_step, 6)
                for s in range(2):
                    pool.wait_ge(hots_ready, turn * TI + (s + 1) * T)
                    pool.sem_inc(pool_steps, 1)
                    side = slice(s * T, (s + 1) * T)
                    nc.gpsimd.tensor_tensor(keys[:, side], keys_next[:, side], clamped[:, side], ALU.add).then_inc(keys_ready, 1)
                pool.wait_ge(keys_ready, turn * 2 + 2)
                pool.sem_inc(pool_steps, 1)

            with pool.Fori(0, ITEMS) as item:
                item_turns(pool, item, turn_count, lambda w, turn, at: key_turn(item, w, turn, at))

            total = pool.snap(**all_turns(turn_count))
            pool.wait_ge(counts_added, total * 2 + 2)
            pool.sem_inc(pool_steps, 1)
            for c in range(DEG_V):
                nc.gpsimd.tensor_copy(counts_b[:, c, :], countsT[:, c, 0:CW]).then_inc(counts_b_ready, 1)
            pool.wait_ge(deg_max_ready, 1)
            nc.gpsimd.partition_all_reduce(deg_max_all, deg_max, P, bass.bass_isa.ReduceOp.max).then_inc(g_chain, 1)
            pool.wait_ge(g_chain, 3)
            nc.gpsimd.tensor_copy(deg_max_i, deg_max_all).then_inc(deg_max_known, 1)

            pool.wait_ge(g_ready, 1)
            pool.wait_ge(paths_in, 48)
            steps = [0]

            def step(ins):
                steps[0] += 1
                ins.then_inc(path_step, 1)
                pool.wait_ge(path_step, steps[0])

            def scalar(o, a, v, op):
                step(nc.gpsimd.tensor_scalar(o, a, v, None, op))

            def both(o, a, b, op):
                step(nc.gpsimd.tensor_tensor(o, a, b, op))

            def count_before(flags):
                a, b = running
                step(nc.gpsimd.memset(a, 0.0))
                step(nc.gpsimd.memset(b, 0.0))
                step(nc.gpsimd.tensor_copy(a[:, NP + 1:2 * NP], flags[:, 0:NP - 1]))
                shift = 1
                while shift < NP:
                    both(b[:, NP:2 * NP], a[:, NP:2 * NP], a[:, NP - shift:2 * NP - shift], ALU.add)
                    a, b = b, a
                    shift *= 2
                return a[:, NP:2 * NP]

            step(nc.gpsimd.iota(spread.bitcast(i32), pattern=[[0, NP]], base=0, channel_multiplier=1))
            step(nc.gpsimd.tensor_copy(partition, spread[:, 0:1].bitcast(i32)))
            step(nc.gpsimd.iota(spread.bitcast(i32), pattern=[[1, NP]], base=0, channel_multiplier=0))
            step(nc.gpsimd.tensor_copy(number, spread.bitcast(i32)))
            step(nc.gpsimd.tensor_copy(path_rows, path_rows_i.rearrange("p (n c) -> p n c", c=3)))
            step(nc.gpsimd.tensor_copy(path_cols, path_cols_i))
            segments = D // U
            scalar(key_row, path_rows[:, :, 0], float(segments), ALU.mult)
            both(key_row, key_row, path_rows[:, :, 1], ALU.add)
            scalar(key_col, path_cols[:, 0:1], float(segments), ALU.mult)
            both(key_col, key_col, path_cols[:, 1:2], ALU.add)
            scalar(same, key_row, key_col, ALU.is_equal)
            scalar(before, number, partition, ALU.is_gt)
            both(before, before, same, ALU.mult)
            step(nc.gpsimd.partition_all_reduce(repeats, before, P, bass.bass_isa.ReduceOp.add))
            scalar(repeats, repeats, 1.0, ALU.min)
            scalar(first, repeats, -1.0, ALU.mult)
            scalar(first, first, 1.0, ALU.add)
            rank = count_before(repeats)
            scalar(merged, rank, float(PG), ALU.is_lt)
            both(merged, merged, repeats, ALU.mult)
            scalar(repeats, merged, -1.0, ALU.mult)
            scalar(repeats, repeats, 1.0, ALU.add)
            place = count_before(repeats)
            both(kept, place[:, NP - 1:NP], repeats[:, NP - 1:NP], ALU.add)
            both(spread, number, place, ALU.subtract)
            scalar(spread, spread, kept, ALU.add)
            both(spread, spread, merged, ALU.mult)
            both(place, place, repeats, ALU.mult)
            both(spread, spread, place, ALU.add)
            ranks = place
            step(nc.gpsimd.tensor_copy(ranks, spread))
            for r in range(1, NP):
                jump = position(r) - position(r - 1) - 1
                if jump:
                    step(nc.gpsimd.tensor_scalar(before, ranks, float(r), float(jump), ALU.is_ge, ALU.mult))
                    both(spread, spread, before, ALU.add)
            scalar(before, number, partition, ALU.is_equal)
            both(place_rows[:, 0, :], before, spread, ALU.mult)
            both(same, same, first, ALU.mult)
            step(nc.gpsimd.tensor_tensor(place_rows[:, 1, :], same, spread, ALU.mult))
            pool.sem_inc(place_rows_ready, 1)
            pool.wait_ge(places_ready, 1)
            for k in range(3):
                step(nc.gpsimd.tensor_copy(path_vals[:, k:k + 1], path_cols[:, k:k + 1]))
            scalar(key_col, partition, float(NP), ALU.is_lt)
            both(path_vals[:, 3:4], places[:, 1:2], key_col, ALU.mult)
            scalar(spread, number, places[:, 0:1], ALU.is_equal)
            for k in range(5):
                scalar(laid[:, k, :], spread, path_vals[:, k:k + 1], ALU.mult)
            step(nc.gpsimd.partition_all_reduce(laid_sum, laid, P, bass.bass_isa.ReduceOp.add))
            step(nc.gpsimd.tensor_copy(coef[:, :], laid_sum[:, 4, :]))
            for k in range(2):
                scalar(i12[0:1, :, k], laid_sum[0:1, k, :], float(U), ALU.mult)
            scalar(i3[0:1, :], laid_sum[0:1, 2, :], float(U), ALU.mult)
            scalar(slot_at[0:1, :].rearrange("a (g n) -> a g n", g=G),
                   laid_sum[0:1, 3, :].rearrange("a (g n) -> a g n", g=G)[:, :, SURE:PG], float(U), ALU.mult)
            step(nc.gpsimd.tensor_copy(n_kept, kept[0:1, :]))
            pool.sem_inc(paths_ready, 1)

            pool.wait_ge(agg_summed, C)
            for i in range(2):
                nc.gpsimd.memset(q[i][:, :, SURE:PG, :], 0.0).then_inc(q_zeroed, 1)

            pool.wait_ge(meta_ready, 1)
            for i in range(2):
                pool.wait_ge(h2_stored[i], 16 * (C // 2))
            pool.wait_ge(xs_stored, 16 * C)
            pool.wait_ge(out_added, 16)
            pool.wait_ge(summed, TURN)
            pool.sem_inc(s_free, 1)
            turn_count = counter(pool, "pool_turn")
            rows = [counter(pool, f"pool_row{s}") for s in range(2)]
            late_row = counter(pool, "pool_late_row")
            slot_regs = [pool.alloc_register(f"slot_{n}") for n in range(PG)]
            i3_regs = [pool.alloc_register(f"i3_{n}") for n in range(PG)]

            def clear_sums(turn):
                pool.wait_ge(out_added, turn * 32 + 32)
                pool.sem_inc(pool_steps, 1)
                pool.sem_clear(mixed)
                nc.gpsimd.memset(acc[:, :], 0.0)
                nc.gpsimd.memset(acc_odd, 0.0).then_inc(mixed, 1)
                return 1

            def scale_last(r, to):
                at, n = position(r), position(r) // PG * (PG - SURE) + position(r) % PG - SURE
                slot = pool.snap(slot_regs[n], min_val=0, max_val=(NP - 1) * U)
                nc.gpsimd.tensor_tensor(to[:, at * U:(at + 1) * U], S[:, ds(slot, U)],
                                        coef[:, at:at + 1].broadcast_to([P, U]), ALU.mult).then_inc(mixed, 1)

            def scale_sure(g, to):
                c = coef[:, g * PG:g * PG + SURE].rearrange("p (n a) -> p n a", a=1).broadcast_to([P, SURE, U])
                a, b = g * PG * U, (g * PG + SURE) * U
                nc.gpsimd.tensor_tensor(to[:, a:b].rearrange("p (n u) -> p n u", u=U),
                                        S[:, a:b].rearrange("p (n u) -> p n u", u=U), c, ALU.mult).then_inc(mixed, 1)

            def add_paths(g, first, end, scaled, step):
                pool.load(i3_regs, i3[0:1, g * PG:(g + 1) * PG])
                for n in range(first, end):
                    i3_at = pool.snap(i3_regs[n], min_val=0, max_val=D - U)
                    into = (acc[:, ds(i3_at, U)], acc_odd[:, ds(i3_at, U)])[n % 2]
                    pool.wait_ge(mixed, step if n == first else step - 1)
                    nc.gpsimd.tensor_tensor(into, into, scaled[:, (g * PG + n) * U:(g * PG + n + 1) * U], ALU.add).then_inc(mixed, 1)
                    step += 1
                pool.wait_ge(mixed, step)
                return step

            def add_first_side(step):
                nc.gpsimd.tensor_tensor(acc[:, :], acc[:, :], acc_odd, ALU.add).then_inc(mixed, 1)
                pool.wait_ge(mixed, step + 1)
                row = pool.snap(rows[0], min_val=0, max_val=N)
                pool.dma_start(out[ds(row, M), :], acc[0:M, :], accum_op=ALU.add).then_inc(out_added, 16)
                pool.reg_mov(late_row, rows[1])

            def mix(turn):
                step = clear_sums(turn)
                pool.load(slot_regs, slot_at[0:1, :])
                pool.wait_ge(saved, turn * G + G)
                pool.sem_inc(pool_steps, 1)
                for r in reversed(range(G * SURE, NP)):
                    scale_last(r, S)
                    step += 1
                    pool.wait_ge(mixed, step)
                for g in range(G):
                    scale_sure(g, S)
                    step = add_paths(g, 0, PG, S, step + 1)
                pool.sem_inc(s_free, 1)
                add_first_side(step)

            def mix_last(turn):
                step = clear_sums(turn)
                pool.load(slot_regs, slot_at[0:1, :])
                pool.wait_ge(multiplied, group_before(turn, G - 1))
                scaled = x1_mem[:, 0:NP * U]
                for g in range(G):
                    pool.wait_ge(saved, turn * G + (g + 1))
                    pool.sem_inc(pool_steps, 1)
                    scale_sure(g, scaled)
                    step = add_paths(g, 0, SURE, scaled, step + 1)
                for r in reversed(range(G * SURE, NP)):
                    scale_last(r, scaled)
                    step += 1
                for g in range(G):
                    step = add_paths(g, SURE, PG, scaled, step)
                add_first_side(step)

            def add_second_side(turn):
                row = pool.snap(late_row, min_val=0, max_val=N)
                pool.wait_ge(out_added, turn * 32 + 16)
                pool.sem_inc(pool_steps, 1)
                pool.dma_start(out[ds(row, M), :], acc[M:P, :], accum_op=ALU.add).then_inc(out_added, 16)

            def gather_turn(item, window, turn, at):
                for j in range(2):
                    pool.wait_ge(multiplied, group_before(turn, j * G + G - 1))
                    now = src_now[:, 2 * T0[j]:2 * (T0[j] + TB[j])]
                    src = src_16[:, :].rearrange("p (b t) -> p b t", t=T)[:, ds(2 * item, 2), T0[j]:T0[j] + TB[j]]
                    nc.gpsimd.tensor_copy(now.rearrange("p (s t) -> p s t", s=2), src).then_inc(idx_copied, 1)
                    pool.wait_ge(idx_copied, turn * 2 + j + 1)
                    pool.sem_inc(pool_steps, 1)
                    for t in range(2 * TB[j]):
                        pool.indirect_dma_start(x1[j][:, t, :], None, h2_dram[:, :],
                                                bass.IndirectOffsetOnAxis(ap=now[:, t:t + 1].bitcast(u32), axis=0)
                                                ).then_inc(x1_in[j], 16)
                    if j == 0:
                        add_second_side(turn)
                mix(turn)
                keep_rows(pool, rows, at, window)

            with pool.Fori(0, ITEMS) as item:
                item_turns(pool, item, turn_count, lambda w, turn, at: gather_turn(item, w, turn, at), bases=True)
            total = pool.snap(**all_turns(turn_count))
            add_second_side(total)
            mix_last(total)
            pool.wait_ge(out_added, total * 32 + 48)
            pool.sem_inc(pool_steps, 1)
            row = pool.snap(late_row, min_val=0, max_val=N)
            pool.dma_start(out[ds(row, M), :], acc[M:P, :], accum_op=ALU.add).then_inc(out_added, 16)
            pool.wait_ge(out_added, total * 32 + 64)

        @block.vector
        def _(dve):
            chain = [0]

            def link(ins):
                chain[0] += 1
                ins.then_inc(v_chain, 1)
                dve.wait_ge(v_chain, chain[0])

            dve.wait_ge(iota_done, 1)
            nc.vector.tensor_copy(iota_h, iota_i[:, 0:KW]).then_inc(consts_ready, 1)
            nc.vector.tensor_scalar(shift_w[:, :], iota_i[:, 0:WINDOWS], float(M), None, ALU.mult).then_inc(consts_ready, 1)
            nc.vector.tensor_copy(iota_f[:, :], iota_i[:, 0:M]).then_inc(consts_ready, 1)

            dve.wait_ge(idx_in, 64)
            nc.vector.tensor_copy(src_f, src_i)
            link(nc.vector.tensor_scalar(tmp_c.bitcast(i32), src_i, 7, None, ALU.arith_shift_right))
            link(nc.vector.tensor_scalar(src_chunk, tmp_c.bitcast(i32), float(M), None, ALU.mult))
            nc.vector.scalar_tensor_tensor(src_row, src_chunk, float(-P // M), src_f, ALU.mult, ALU.add)
            nc.vector.scalar_tensor_tensor(minus_row, src_chunk, float(P // M), src_f, ALU.mult, ALU.subtract).then_inc(consts_ready, 1)
            nc.vector.tensor_copy(src_16[:, :], src_i)
            link(nc.vector.tensor_copy(dst_f[:, :], dst_i))
            link(nc.vector.tensor_scalar(tmp_c, dst_f[:, :], -1.0, None, ALU.mult))
            nc.vector.tensor_reduce(span[:, 0:SIDES], tmp_c.rearrange("p (i t) -> p i t", t=T), AX.X, ALU.max)
            link(nc.vector.tensor_scalar(dst_i.bitcast(fp32), dst_f[:, :], float(NOWHERE), None, ALU.is_lt))
            link(nc.vector.tensor_tensor(tmp_c, dst_i.bitcast(fp32), dst_f[:, :], ALU.mult))
            nc.vector.tensor_reduce(span[:, SIDES:2 * SIDES], tmp_c.rearrange("p (i t) -> p i t", t=T), AX.X,
                                    ALU.max).then_inc(span_ready, 1)

            dve.wait_ge(span_reduced, 1)
            link(nc.vector.tensor_scalar(base_f[:, :], span_all[:, 0:SIDES], -1.0, None, ALU.mult))
            link(nc.vector.tensor_tensor(tmp_c[:, 0:SIDES], span_all[:, SIDES:2 * SIDES], base_f[:, :], ALU.subtract))
            link(nc.vector.tensor_reduce(tmp_c[:, SIDES:SIDES + ITEMS],
                                         tmp_c[:, 0:SIDES].rearrange("p (i s) -> p i s", s=2), AX.X, ALU.max))
            nc.vector.tensor_copy(meta[:, 0:SIDES], base_f[:, :])
            nc.vector.tensor_copy(meta[:, SIDES:SIDES + ITEMS], tmp_c[:, SIDES:SIDES + ITEMS]).then_inc(meta_ready, 1)

            dve.wait_ge(x_in, 32)
            for c in range(C):
                last = nc.vector.bn_stats(stats[:, c, :], xs[:, c, :])
            link(last)
            for c in range(C):
                last = nc.vector.bn_aggr(mv[:, c, :], stats[:, c, :])
            link(last)
            nc.vector.tensor_scalar(rstd, mv[:, :, 1], EPS, None, ALU.add).then_inc(var_ready, 1)

            dve.wait_ge(root_ready, 1)
            link(nc.vector.reciprocal(rstd, rstd))
            link(nc.vector.tensor_tensor(shift, mv[:, :, 0], rstd, ALU.mult))
            nc.vector.tensor_scalar(shift, shift, -1.0, None, ALU.mult).then_inc(norm_ready, 1)

            dve.wait_ge(consts_ready, 4)
            dve.wait_ge(countsT_init, C)
            dve.sem_inc(hots_ready, TI)
            turn_count = counter(dve, "dve_turn0")
            rows = [counter(dve, f"dve_row{s}") for s in range(2)]

            def add_counts(s, half):
                row = dve.snap(rows[s], min_val=0, max_val=N)
                dve.wait_ge(hots_used, half * T + TI)
                dve.wait_ge(counts_added, half + 1)
                to = countsT[:, :, ds(row, M)]
                nc.vector.tensor_tensor(to, key_sums[s].rearrange("p (c n) -> p c n", n=M), to,
                                        ALU.add).then_inc(counts_added, 1)

            def key_hot_turn(item, window, turn, at):
                for s in range(2):
                    dve.wait_ge(keys_ready, turn * 2 + (s + 1))
                    for t in range(T):
                        n = s * T + t
                        dve.wait_ge(hots_used, turn * TI + (n + 1 + TI - RING))
                        if t >= ROWS_A:
                            nc.vector.tensor_scalar(row_hot[s][:, t, :], iota_h[:, 0:P], src_row[:, ds(item * TI + n, 1)],
                                                    None, ALU.is_equal)
                        nc.vector.tensor_scalar(key_hot[:, n % RING, :], iota_h, keys[:, n:n + 1], None,
                                                ALU.is_equal).then_inc(hots_ready, 1)
                        if t == LATER:
                            add_counts(1 - s, turn * 2 + s)
                            if s == 0:
                                keep_rows(dve, rows, at, window)

            with dve.Fori(0, ITEMS) as item:
                item_turns(dve, item, turn_count, lambda w, turn, at: key_hot_turn(item, w, turn, at), bases=True)
            total = dve.snap(**all_turns(turn_count))
            add_counts(1, total * 2)

            dve.wait_ge(counts_added, total * 2 + 2)
            nc.vector.tensor_reduce(deg[:, 0:DEG_V], countsT[:, 0:DEG_V, :], AX.X, ALU.add).then_inc(g_ready, 1)
            dve.wait_ge(g_ready, 1)
            dve.wait_ge(degrees_ready, C - DEG_V)
            dve.sem_inc(multiplied, TURN)
            nc.vector.tensor_scalar(dis, deg, 1.0, None, ALU.mult).then_inc(var_ready, 1)
            nc.vector.tensor_reduce(deg_max, deg, AX.X, ALU.max).then_inc(deg_max_ready, 1)
            dve.wait_ge(root_ready, 2)
            nc.vector.reciprocal(dis, dis).then_inc(g_ready, 1)
            dve.wait_ge(g_ready, 2)
            dve.wait_ge(hw_saved, C + 1)
            for c in range(C + 3):
                if c < C:
                    nc.vector.tensor_scalar(hw[:, c + 1, :], hw[:, c + 1, :], dis[:, c:c + 1], None, ALU.mult).then_inc(g_ready, 1)
                m = c - 2
                if 0 <= m < C:
                    dve.wait_ge(parts_in[0], m + 1)
                    if m >= 4:
                        dve.wait_ge(parts_in[2], m - 3)
                    nc.vector.tensor_tensor(rests[m % 4], hw[:, m + 1, :], parts[0][:, m, :], ALU.subtract).then_inc(rest_ready, 1)
                m = c - 3
                if 0 <= m < C:
                    dve.wait_ge(parts_in[1], m + 1)
                    nc.vector.tensor_tensor(parts[2][:, m, :], rests[m % 4], parts[1][:, m, :], ALU.subtract).then_inc(parts_in[2], 1)

            for c in range(C):
                if c == C // 2:
                    dve.wait_ge(place_rows_ready, 1)
                    nc.vector.tensor_reduce(places, place_rows, AX.X, ALU.add).then_inc(places_ready, 1)
                dve.wait_ge(y_ready, c + 1)
                nc.vector.tensor_tensor(xs[:, c, :], xs[:, c, :], y[:, c % 2, :], ALU.add).then_inc(xs_ready, 1)
                dve.wait_ge(xs_ready, 5 * c + 1)
                nc.vector.bn_stats(stats2, xs[:, c, :]).then_inc(xs_ready, 1)
                dve.wait_ge(xs_ready, 5 * c + 2)
                nc.vector.bn_aggr(mv2, stats2).then_inc(xs_ready, 1)
                dve.wait_ge(xs_ready, 5 * c + 3)
                if c >= 2:
                    dve.wait_ge(h2_ready, c - 1)
                nc.vector.tensor_scalar(rs2[:, c % 2, 0:1], mv2[:, 1:2], EPS, None, ALU.add).then_inc(var_ready, 1)
                dve.wait_ge(root_ready, c + 3)
                nc.vector.reciprocal(rs2[:, c % 2, 0:1], rs2[:, c % 2, 0:1]).then_inc(xs_ready, 1)
                dve.wait_ge(xs_ready, 5 * c + 4)
                nc.vector.tensor_scalar(rs2[:, c % 2, 1:2], mv2[:, 0:1], rs2[:, c % 2, 0:1], -1.0, ALU.mult,
                                        ALU.mult).then_inc(xs_ready, 1)

            turn_count = counter(dve, "dve_turn1")
            regs = [dve.alloc_register(f"i12_{n}") for n in range(PG)]

            dve.wait_ge(paths_ready, 1)
            dve.wait_ge(q_zeroed, 2)
            kept_n = dve.value_load(n_kept, min_val=NP - PG, max_val=NP)

            def product(j, s, r1, r2, n):
                a = dve.snap(r1, min_val=0, max_val=D - U)
                b = dve.snap(r2, min_val=0, max_val=D - U)
                slot = q[s % 2][:, 0:2 * TB[j], :, :]
                to = slot[:, :, n, :] if isinstance(n, int) else slot[:, :, ds(n, 1), :].rearrange("p t n u -> p t (n u)")
                return nc.vector.tensor_tensor(to, x1[j][:, :, ds(a, U)], x2[j][:, :, ds(b, U)], ALU.mult)

            def product_turn(window, turn, at):
                for j in range(2):
                    for g in range(G):
                        s = j * G + g
                        for half in (1, 0):
                            p0 = g * PG + half * (PG // 2)
                            dve.load(regs, i12[0:1, p0:p0 + PG // 2, :].rearrange("a n c -> a (n c)"))
                            if half:
                                if g == 0:
                                    dve.wait_ge(x1_in[j], turn * (32 * TB[j]) + 32 * TB[j])
                                    dve.wait_ge(x2_in[j], turn * 32 + 32)
                                dve.wait_ge(summed, group(turn, s - 2))
                                dve.sem_inc(steps_reg, 1)

                            def products(n, count):
                                for m in range(n, n + count):
                                    last = product(j, s, regs[2 * m], regs[2 * m + 1], half * (PG // 2) + m)
                                return last

                            if half:
                                products(0, SURE - PG // 2)
                                for k in range(2):
                                    with dve.If(kept_n > G * SURE + (k * G + g) * PAIR):
                                        products(SURE - PG // 2 + k * PAIR, PAIR)
                            else:
                                last = products(0, PG // 2)
                        last.then_inc(multiplied, 1)

            with dve.Fori(0, ITEMS) as item:
                item_turns(dve, item, turn_count, product_turn)

        @block.scalar
        def _(act):
            act.wait_ge(pads_set, 3)
            act.dma_start(src_i[:, 0:FULL * T].rearrange("p (b t) -> p b t", t=T), src_full).then_inc(idx_in, 16)
            act.dma_start(src_i[0:TAIL, FULL * T:COLS], src_tail).then_inc(idx_in, 16)
            act.dma_start(bias_b, bias.rearrange("(a n) -> a n", a=1).broadcast_to([P, D])).then_inc(small_in, 16)

            act.wait_ge(zeros_set, 2)
            for c in range(C // 2, C):
                nc.scalar.activation(countsT[:, c, :], acc[:, 0:1].broadcast_to([P, AW]), ACT.Copy).then_inc(countsT_cleared, 1)
            act.wait_ge(ident_done, 1)
            act.wait_ge(countsT_cleared, 1 + C - C // 2)
            for c in range(C):
                nc.scalar.activation(countsT[:, c, c * P:(c + 1) * P], ident, ACT.Copy).then_inc(countsT_init, 1)

            for k in range(K):
                act.wait_ge(w_transposed, k + 1)
                nc.scalar.activation(wT[:, k, :], ps[4 + k % 2], ACT.Copy).then_inc(wT_ready, 1)
            act.wait_ge(var_ready, 1)
            nc.scalar.activation(rstd, rstd, ACT.Sqrt).then_inc(root_ready, 1)
            act.wait_ge(norm_ready, 1)
            act.wait_ge(meta_ready, 1)
            act.wait_ge(consts_ready, 4)
            act.wait_ge(zeros_set, 2)
            turn_count = counter(act, "act_turn0")

            def distances(item, window, turn, chain):
                act.wait_ge(chain, turn * 4 + 4)
                for s in range(2):
                    last = nc.scalar.activation(rel[:, 0, s * T:(s + 1) * T], dst_f[:, ds((item * 2 + s) * T, T)],
                                                ACT.Identity, scale=-1.0, bias=base_f[:, ds(item * 2 + s, 1)])
                last.then_inc(chain, 1)
                act.wait_ge(chain, turn * 4 + 5)
                nc.scalar.activation(rel[:, 1, :], rel[:, 0, :], ACT.Identity,
                                     bias=shift_w[:, ds(window, 1)]).then_inc(chain, 1)
                act.wait_ge(chain, turn * 4 + 6)

            def destinations(j, hots, turn, chain, ready):
                for s in range(2):
                    for t in range(TB[j]):
                        at = s * T + T0[j] + t
                        last = nc.scalar.activation(hots[:, s * TB[j] + t, :], iota_f[:, :], ACT.Abs, bias=rel[:, 1, at:at + 1])
                last.then_inc(chain, 1)
                act.wait_ge(chain, turn * 4 + (7 + j))
                nc.scalar.activation(hots, hots, ACT.Relu, scale=-1.0, bias=1.0).then_inc(ready, 1)

            def save_features(c):
                act.wait_ge(hw_summed, c + 1)
                to = hw[:, c, :] if isinstance(c, int) else hw[:, ds(c, 1), :].rearrange("p c d -> p (c d)")
                nc.scalar.activation(to, ps[7], ACT.Copy).then_inc(hw_saved, 1)

            def normalise(c):
                act.wait_ge(h1_transposed, c + 1)
                nc.scalar.activation(h1, xs[:, ds(c, 1), :].rearrange("p c d -> p (c d)"), ACT.Relu,
                                     bias=shift[:, ds(c, 1)], scale=rstd[:, ds(c, 1)]).then_inc(h1_ready, 1)

            def save_transposed(c):
                act.wait_ge(h1_transposed, c + 2)
                act.wait_ge(hw_summed, c + 1)
                nc.scalar.activation(h1T, ps[6], ACT.Copy).then_inc(h1T_ready, 1)

            def row_hot_turn(item, window, turn, at):
                for s in range(2):
                    act.wait_ge(hots_used, turn * TI + (s + 1) * T)
                    for t in range(ROWS_A):
                        last = nc.scalar.activation(row_hot[s][:, t, :], iota_h[:, 0:P], ACT.Abs,
                                                    bias=minus_row[:, ds(item * TI + (s * T + t), 1)])
                    last.then_inc(a_chain0, 1)
                    act.wait_ge(a_chain0, turn * 2 + (s + 1))
                    nc.scalar.activation(row_hot[s][:, 0:ROWS_A, :], row_hot[s][:, 0:ROWS_A, :], ACT.Relu, scale=-1.0,
                                         bias=1.0).then_inc(rows_ready, 1)

            with act.Fori(0, C) as item:
                normalise(item)
                item_turns(act, item, turn_count, lambda w, turn, at: row_hot_turn(item, w, turn, at))
                save_features(item)
                save_transposed(item)
            with act.Fori(C, ITEMS) as item:
                item_turns(act, item, turn_count, lambda w, turn, at: row_hot_turn(item, w, turn, at))
            save_features(C)

            total = act.snap(**all_turns(turn_count))
            act.wait_ge(counts_added, total * 2 + 2)
            for c in range(DEG_V, C):
                nc.scalar.activation(counts_b[:, c, :], countsT[:, c, 0:CW], ACT.Copy, accum_out=deg[:, c:c + 1]).then_inc(degrees_ready, 1)
            act.wait_ge(var_ready, 2)
            nc.scalar.activation(dis, dis, ACT.Sqrt).then_inc(root_ready, 1)
            for c in range(C + 2):
                if c < C:
                    act.wait_ge(g_ready, 3 + c)
                    nc.scalar.activation(parts[0][:, c, :], hw[:, c + 1, :], ACT.Copy).then_inc(parts_in[0], 1)
                m = c - 2
                if m >= 0:
                    act.wait_ge(rest_ready, m + 1)
                    nc.scalar.activation(parts[1][:, m, :], rests[m % 4], ACT.Copy).then_inc(parts_in[1], 1)
            act.wait_ge(parts_in[2], C)
            for c in range(C):
                rows = P if c < C - 1 else LAST
                act.wait_ge(agg_summed, c + 1)
                nc.scalar.activation(y[:, c % 2, :], ps[agg_bank(c)], ACT.Relu, scale=dis[:, c:c + 1]).then_inc(y_ready, 1)
                act.wait_ge(var_ready, c + 3)
                nc.scalar.activation(rs2[:, c % 2, 0:1], rs2[:, c % 2, 0:1], ACT.Sqrt).then_inc(root_ready, 1)
                act.wait_ge(xs_ready, 5 * c + 5)
                if c >= 2:
                    act.wait_ge(h2_stored[c % 2], 16 * (c // 2))
                nc.scalar.activation(h2[:, c % 2, :], xs[:, c, :], ACT.Relu, bias=rs2[:, c % 2, 1:2],
                                     scale=rs2[:, c % 2, 0:1]).then_inc(h2_ready, 1)
                act.dma_start(out[c * P:c * P + rows, :], xs[0:rows, c, :]).then_inc(xs_stored, 16)
                act.wait_ge(h2_ready, c + 1)
                act.dma_start(h2_dram[c * P:c * P + rows, :], h2[0:rows, c % 2, :]).then_inc(h2_stored[c % 2], 16)

            act.sem_inc(a_chain1, 4)
            turn_count = counter(act, "act_turn1")


            def save(turn):
                act.wait_ge(s_free, turn + 1)
                for g in range(G):
                    act.wait_ge(summed, group_before(turn, G + g))
                    ins = nc.scalar.activation(S[:, g * PG * U:(g + 1) * PG * U], ps[g], ACT.Copy)
                    ins.then_inc(saved, 1)

            def sum_turn(item, window, turn, at):
                distances(item, window, turn, a_chain1)
                for j in range(2):
                    act.wait_ge(summed, group_before(turn, j * G + G - 1))
                    destinations(j, hot[j].rearrange("p s t n -> p (s t) n"), turn, a_chain1, hot_ready)
                    if j == 0:
                        save(turn)

            with act.Fori(0, ITEMS) as item:
                item_turns(act, item, turn_count, lambda w, turn, at: sum_turn(item, w, turn, at))
            save(act.snap(**all_turns(turn_count)))

        @block.tensor
        def _(pe):
            pe.wait_ge(zeros_set, 2)
            pe.sem_inc(counts_added, 1)
            pe.sem_inc(h1_transposed, 1)
            pe.sem_inc(h1T_ready, 1)
            nc.tensor.matmul(ps[7], acc[:, 0:P], acc[:, :], start=True, stop=True).then_inc(hw_summed, 1)
            for a in range(0, KW, BANK):
                b = min(a + BANK, KW)
                last = nc.tensor.matmul(key_sums[1][:, a:b], acc[:, 0:P], acc[:, 0:b - a], start=True, stop=True)
            last.then_inc(hots_used, TI)

            pe.wait_ge(ident_done, 1)
            pe.wait_ge(w_in, 16)
            for k in range(K):
                if k >= 2:
                    pe.wait_ge(wT_ready, k - 1)
                for o in range(K):
                    last = nc.tensor.transpose(ps[4 + k % 2][:, o * P:(o + 1) * P], w_rows[:, o, k * P:(k + 1) * P], ident)
                last.then_inc(w_transposed, 1)

            pe.wait_ge(meta_ready, 1)
            pe.wait_ge(wT_ready, K)
            pe.wait_ge(small_in, 16)
            turn_count = counter(pe, "pe_turn0")

            def transpose_features(c):
                pe.wait_ge(h1_ready, c + 1)
                pe.wait_ge(h1T_ready, c + 1)
                for k in range(K):
                    last = nc.tensor.transpose(ps[6][:, k * P:(k + 1) * P], h1[:, k * P:(k + 1) * P], ident)
                last.then_inc(h1_transposed, 1)

            def multiply_features(c):
                pe.wait_ge(hw_saved, c + 1)
                nc.tensor.matmul(ps[7], first_row, bias_b, start=True, stop=False)
                pe.wait_ge(h1T_ready, c + 2)
                for k in range(K):
                    last = nc.tensor.matmul(ps[7], h1T[:, k * P:(k + 1) * P], wT[:, k, :], start=False, stop=(k == K - 1))
                last.then_inc(hw_summed, 1)

            def count_turn(window, turn, at):
                for s in range(2):
                    pe.wait_ge(rows_ready, turn * 2 + (s + 1))
                    pe.wait_ge(counts_added, turn * 2 + (s + 1))
                    for t in range(T):
                        n = s * T + t
                        pe.wait_ge(hots_ready, turn * TI + (n + 1 + TI))
                        for a in range(0, KW, BANK):
                            b = min(a + BANK, KW)
                            last = nc.tensor.matmul(key_sums[s][:, a:b], row_hot[s][:, t, :], key_hot[:, n % RING, a:b],
                                                    start=(t == 0), stop=(t == T - 1))
                        last.then_inc(hots_used, 1)

            with pe.Fori(0, C) as item:
                transpose_features(item)
                item_turns(pe, item, turn_count, count_turn)
                multiply_features(item)
            with pe.Fori(C, ITEMS) as item:
                item_turns(pe, item, turn_count, count_turn)

            total = pe.snap(**all_turns(turn_count))
            pe.wait_ge(counts_added, total * 2 + 2)
            for n in range(24):
                nc.tensor.matmul(ps[4][0:M, 0:COLS], iota_f[:, :], dst_f[:, :], start=True, stop=True)

            pe.wait_ge(counts_b_ready, DEG_V)
            pe.wait_ge(degrees_ready, C - DEG_V)
            pe.wait_ge(deg_max_known, 1)
            largest = pe.value_load(deg_max_i[0:1, :], min_val=0, max_val=E + 1)

            def aggregate(counts, features):
                def add(c, m):
                    for rhs in features:
                        last = nc.tensor.matmul(ps[agg_bank(c)], counts[:, m, c * P:(c + 1) * P], rhs[:, m, :],
                                                start=(m == 0 and rhs is features[0]),
                                                stop=(m == C - 1 and rhs is features[-1]))
                    return last

                for m in range(C):
                    pe.wait_ge(parts_in[2], m + 1)
                    for c in range(AHEAD):
                        last = add(c, m)
                        if m == C - 1:
                            last.then_inc(agg_summed, 1)
                for c in range(AHEAD, C):
                    if c >= AHEAD + 4:
                        pe.wait_ge(y_ready, c - 3)
                    for m in range(C):
                        last = add(c, m)
                    last.then_inc(agg_summed, 1)

            with pe.If(largest < EXACT + 1):
                aggregate(counts_b, parts)
            with pe.If(largest > EXACT):
                aggregate(countsT, [hw[:, 1:C + 1, :]])

            turn_count = counter(pe, "pe_turn1")
            for g in range(G):
                last = nc.tensor.matmul(ps[g], acc[:, 0:P], acc[:, :], start=True, stop=True)
            last.then_inc(summed, TURN)

            pe.wait_ge(x1_in[0], 32 * TB[0])
            for n in range(12):
                nc.tensor.matmul(ps[4][0:M, 0:COLS], iota_f[:, :], dst_f[:, :], start=True, stop=True)

            def sum_turn(window, turn, at):
                for j in range(2):
                    pe.wait_ge(hot_ready, turn * 2 + (j + 1))
                    for g in range(G):
                        slot = j * G + g
                        pe.wait_ge(multiplied, group(turn, slot))
                        if slot == 0:
                            pe.wait_ge(saved, turn * G + G)
                        for t in range(TB[j]):
                            for s in range(2):
                                last = nc.tensor.matmul(ps[g][s * M:(s + 1) * M, :], hot[j][:, s, t, :],
                                                        q[slot % 2][:, s * TB[j] + t, :, :].rearrange("p n u -> p (n u)"),
                                                        start=(j == 0 and t == 0), stop=(j == 1 and t == TB[j] - 1))
                        last.then_inc(summed, 1)

            with pe.Fori(0, ITEMS) as item:
                item_turns(pe, item, turn_count, sum_turn)


_INS = ["x", "src", "dst", "edge_attr_512", "L0_gnn_W", "L0_gnn_b", "L1_gnn_path_coeffs", "L1_gnn_path_indices"]


def kernel(**inputs):
    import numpy as _np
    import concourse.bacc as _bacc
    from concourse import mybir as _mybir
    from concourse.bass_utils import run_bass_kernel_spmd as _run

    nc = _bacc.Bacc("TRN2", target_bir_lowering=False, num_devices=1)
    arrays, args = {}, []
    for name in _INS:
        a = _np.ascontiguousarray(inputs[name])
        arrays[f"in_{name}"] = a
        args.append(nc.dram_tensor(f"in_{name}", a.shape, _mybir.dt.from_np(a.dtype), kind="ExternalInput").ap())
    n, d = arrays["in_x"].shape
    args.append(nc.dram_tensor("out_0", (n + 64, d), _mybir.dt.float32, kind="ExternalOutput").ap())
    gnn_layers_kernel(nc, *args)
    r = _run(nc, [arrays], core_ids=[0])
    return r.results[0]["out_0"][:n]
```
